# Optimizing a Trainium2 kernel written in Bass

```python
import numpy as np
import jax
import jax.numpy as jnp

def _softmax(x, axis=-1):
    return jax.nn.softmax(x, axis=axis)

def _gelu(x):
    return jax.nn.gelu(x, approximate=True)

def _silu(x):
    return jax.nn.silu(x)

def _sigmoid(x):
    return jax.nn.sigmoid(x)

def _layernorm(x, axis=-1, eps=1e-05):
    m = jnp.mean(x, axis=axis, keepdims=True)
    v = jnp.var(x, axis=axis, keepdims=True)
    return (x - m) / jnp.sqrt(v + eps)

def _scatter_add(tgt, idx, src, axis=0):
    return tgt.at[idx].add(src)

def _segment_sum(src, seg, n):
    return jax.ops.segment_sum(src, seg, n)
kernel_name = 'mk_macaron_d2_jaxref_r8_441be5'

def setup_inputs(seed: int=0):
    np.random.seed(seed)
    _w = jnp.asarray

    def _L0_attn_setup():
        import jax, jax.numpy as jnp
        import numpy as np
        DIM = 128
        HEADS = 16
        THS = 0.5
        C = float(np.e) * float(np.sqrt(1.0 / DIM))

        def _pm_c(key, shape):
            return jnp.where(jax.random.bernoulli(key, 0.5, shape), C, -C).astype(jnp.float32)
        key = jax.random.key(seed)
        ks = jax.random.split(key, 7)
        b, n = (2, 256)
        return {'x': jax.random.normal(ks[0], (b, n, DIM), jnp.float32), 'qkv_weight': _pm_c(ks[1], (3 * DIM, DIM)), 'qkv_weight_mask': jax.random.normal(ks[2], (3 * DIM, DIM), jnp.float32), 'out_weight': _pm_c(ks[3], (DIM, DIM)), 'out_weight_mask': jax.random.normal(ks[4], (DIM, DIM), jnp.float32), 'out_bias': _pm_c(ks[5], (DIM,)), 'out_bias_mask': jax.random.normal(ks[6], (DIM,), jnp.float32)}
    _L0_attn_in = _L0_attn_setup()

    def _L0_ffn_setup():
        import jax, jax.numpy as jnp
        import numpy as np
        E = 8
        D = 128
        DO = 128
        R = 64
        H = 32
        B, T = (8, 256)
        key = jax.random.key(seed)
        ks = jax.random.split(key, 12)
        s = lambda k, shape, fan: jax.random.normal(k, shape, jnp.float32) / np.sqrt(fan)
        return {'x': jax.random.normal(ks[0], (B, T, D), jnp.float32), 'W_base': s(ks[1], (D, DO), D), 'b_base': jnp.zeros((DO,), jnp.float32), 'Wd1': s(ks[2], (E, D, H), D), 'bd1': jnp.zeros((E, H), jnp.float32), 'Wd2': s(ks[3], (E, H, D), H), 'bd2': jnp.zeros((E, D), jnp.float32), 'Wa_down': s(ks[4], (E, D, R), D), 'ba_down': jnp.zeros((E, R), jnp.float32), 'Wa_up': s(ks[5], (E, R, DO), R), 'ba_up': jnp.zeros((E, DO), jnp.float32)}
    _L0_ffn_in = _L0_ffn_setup()

    def _L1_attn_setup():
        import jax, jax.numpy as jnp
        import numpy as np
        from jax import lax
        B, L, D, N, DT_RANK = (2, 256, 128, 16, 64)

        def _scan_op(l, r):
            g_l, h_l = l
            g_r, h_r = r
            return (g_l * g_r, g_r * h_l + h_r)
        key = jax.random.key(seed)
        ks = jax.random.split(key, 8)
        x = jax.random.normal(ks[0], (B, L, D), dtype=jnp.float32)
        conv_kernel = jax.random.normal(ks[1], (3, 1, D), dtype=jnp.float32) * (1.0 / np.sqrt(3.0))
        A_log = jnp.log(jnp.repeat(jnp.arange(1, N + 1, dtype=jnp.float32)[None, :], D, axis=0))
        W_bc = jax.random.normal(ks[2], (D, 2 * N), dtype=jnp.float32) * (1.0 / np.sqrt(D))
        b_bc = jnp.zeros((2 * N,), dtype=jnp.float32)
        Dcoeff = jnp.ones((D,), dtype=jnp.float32)
        W_dt = jax.random.normal(ks[3], (D, DT_RANK), dtype=jnp.float32) * (1.0 / np.sqrt(D))
        b_dt = jnp.zeros((DT_RANK,), dtype=jnp.float32)
        W_dtp = jax.random.normal(ks[4], (DT_RANK, D), dtype=jnp.float32) * (1.0 / np.sqrt(DT_RANK))
        u01 = jax.random.uniform(ks[5], (D,), dtype=jnp.float32, minval=0.001, maxval=0.1)
        b_dtp = u01 + jnp.log(1.0 - jnp.exp(-u01))
        return {'x': x, 'conv_kernel': conv_kernel, 'A_log': A_log, 'W_bc': W_bc, 'b_bc': b_bc, 'Dcoeff': Dcoeff, 'W_dt': W_dt, 'b_dt': b_dt, 'W_dtp': W_dtp, 'b_dtp': b_dtp}
    _L1_attn_in = _L1_attn_setup()

    def _L1_ffn_setup():
        import jax, jax.numpy as jnp
        import numpy as np
        H = 128
        I = 4 * H
        E = 8
        K = 2
        B, S = (2, 128)
        STD = 0.02 / np.sqrt(H)
        key = jax.random.key(seed)
        ks = jax.random.split(key, 8)
        x = jax.random.normal(ks[0], (B, S, H), dtype=jnp.float32)
        gate_w = jax.random.normal(ks[1], (H, E), dtype=jnp.float32) * STD
        bias = jnp.zeros((E,), dtype=jnp.float32)
        up_w = jax.random.normal(ks[2], (E, H, I), dtype=jnp.float32) * STD
        up_b = jnp.zeros((E, I), dtype=jnp.float32)
        down_w = jax.random.normal(ks[3], (E, I, H), dtype=jnp.float32) * STD
        down_b = jnp.zeros((E, H), dtype=jnp.float32)
        sw_up = jax.random.normal(ks[4], (H, I), dtype=jnp.float32) * STD
        sb_up = jnp.zeros((I,), dtype=jnp.float32)
        sw_down = jax.random.normal(ks[5], (I, H), dtype=jnp.float32) * STD
        sb_down = jnp.zeros((H,), dtype=jnp.float32)
        return {'x': x, 'gate_w': gate_w, 'bias': bias, 'up_w': up_w, 'up_b': up_b, 'down_w': down_w, 'down_b': down_b, 'sw_up': sw_up, 'sb_up': sb_up, 'sw_down': sw_down, 'sb_down': sb_down}
    _L1_ffn_in = _L1_ffn_setup()
    _d = {'L0_attn_x': _L0_attn_in['x'], 'L0_attn_qkv_weight': _L0_attn_in['qkv_weight'], 'L0_attn_qkv_weight_mask': _L0_attn_in['qkv_weight_mask'], 'L0_attn_out_weight': _L0_attn_in['out_weight'], 'L0_attn_out_weight_mask': _L0_attn_in['out_weight_mask'], 'L0_attn_out_bias': _L0_attn_in['out_bias'], 'L0_attn_out_bias_mask': _L0_attn_in['out_bias_mask'], 'L0_ffn_W_base': _L0_ffn_in['W_base'], 'L0_ffn_b_base': _L0_ffn_in['b_base'], 'L0_ffn_Wd1': _L0_ffn_in['Wd1'], 'L0_ffn_bd1': _L0_ffn_in['bd1'], 'L0_ffn_Wd2': _L0_ffn_in['Wd2'], 'L0_ffn_bd2': _L0_ffn_in['bd2'], 'L0_ffn_Wa_down': _L0_ffn_in['Wa_down'], 'L0_ffn_ba_down': _L0_ffn_in['ba_down'], 'L0_ffn_Wa_up': _L0_ffn_in['Wa_up'], 'L0_ffn_ba_up': _L0_ffn_in['ba_up'], 'L1_attn_conv_kernel': _L1_attn_in['conv_kernel'], 'L1_attn_A_log': _L1_attn_in['A_log'], 'L1_attn_W_bc': _L1_attn_in['W_bc'], 'L1_attn_b_bc': _L1_attn_in['b_bc'], 'L1_attn_Dcoeff': _L1_attn_in['Dcoeff'], 'L1_attn_W_dt': _L1_attn_in['W_dt'], 'L1_attn_b_dt': _L1_attn_in['b_dt'], 'L1_attn_W_dtp': _L1_attn_in['W_dtp'], 'L1_attn_b_dtp': _L1_attn_in['b_dtp'], 'L1_ffn_gate_w': _L1_ffn_in['gate_w'], 'L1_ffn_bias': _L1_ffn_in['bias'], 'L1_ffn_up_w': _L1_ffn_in['up_w'], 'L1_ffn_up_b': _L1_ffn_in['up_b'], 'L1_ffn_down_w': _L1_ffn_in['down_w'], 'L1_ffn_down_b': _L1_ffn_in['down_b'], 'L1_ffn_sw_up': _L1_ffn_in['sw_up'], 'L1_ffn_sb_up': _L1_ffn_in['sb_up'], 'L1_ffn_sw_down': _L1_ffn_in['sw_down'], 'L1_ffn_sb_down': _L1_ffn_in['sb_down']}
    _x0 = _d['L0_attn_x']
    _d['L0_attn_x'] = jax.random.normal(jax.random.fold_in(jax.random.key(seed), 1), (8, 512, 128), dtype=_x0.dtype)
    del _x0
    return _d

def reference(L0_attn_x, L0_attn_qkv_weight, L0_attn_qkv_weight_mask, L0_attn_out_weight, L0_attn_out_weight_mask, L0_attn_out_bias, L0_attn_out_bias_mask, L0_ffn_W_base, L0_ffn_b_base, L0_ffn_Wd1, L0_ffn_bd1, L0_ffn_Wd2, L0_ffn_bd2, L0_ffn_Wa_down, L0_ffn_ba_down, L0_ffn_Wa_up, L0_ffn_ba_up, L1_attn_conv_kernel, L1_attn_A_log, L1_attn_W_bc, L1_attn_b_bc, L1_attn_Dcoeff, L1_attn_W_dt, L1_attn_b_dt, L1_attn_W_dtp, L1_attn_b_dtp, L1_ffn_gate_w, L1_ffn_bias, L1_ffn_up_w, L1_ffn_up_b, L1_ffn_down_w, L1_ffn_down_b, L1_ffn_sw_up, L1_ffn_sb_up, L1_ffn_sw_down, L1_ffn_sb_down):

    def _L0_attn_ref(x, qkv_weight, qkv_weight_mask, out_weight, out_weight_mask, out_bias, out_bias_mask):
        import jax, jax.numpy as jnp
        import numpy as np
        DIM = 128
        HEADS = 16
        THS = 0.5
        C = float(np.e) * float(np.sqrt(1.0 / DIM))

        def _pm_c(key, shape):
            return jnp.where(jax.random.bernoulli(key, 0.5, shape), C, -C).astype(jnp.float32)
        b, n, _ = x.shape
        h, d = (HEADS, DIM // HEADS)
        dt = x.dtype
        g_qkv = (jax.nn.sigmoid(qkv_weight_mask) > THS).astype(dt)
        qkv = jnp.einsum('bnk,ok->bno', x, g_qkv * qkv_weight)
        qkv = qkv.reshape(b, n, 3, h, d)
        q, k, v = (jnp.transpose(qkv[:, :, i], (0, 2, 1, 3)) for i in range(3))
        scale = DIM ** (-0.5)
        dots = jnp.einsum('bhid,bhjd->bhij', q, k) * scale
        attn = jax.nn.softmax(dots, axis=-1)
        out = jnp.einsum('bhij,bhjd->bhid', attn, v)
        out = jnp.transpose(out, (0, 2, 1, 3)).reshape(b, n, h * d)
        g_w = (jax.nn.sigmoid(out_weight_mask) > THS).astype(dt)
        g_b = (jax.nn.sigmoid(out_bias_mask) > THS).astype(dt)
        out = jnp.einsum('bnk,ok->bno', out, g_w * out_weight) + g_b * out_bias
        return out

    def _L0_ffn_ref(x, W_base, b_base, Wd1, bd1, Wd2, bd2, Wa_down, ba_down, Wa_up, ba_up):
        import jax, jax.numpy as jnp
        import numpy as np
        E = 8
        D = 128
        DO = 128
        R = 64
        H = 32
        B, T = (8, 256)
        base = jnp.einsum('btd,do->bto', x, W_base) + b_base
        h = jax.nn.relu(jnp.einsum('btd,edh->ebth', x, Wd1) + bd1[:, None, None, :])
        recon = jnp.einsum('ebth,ehd->ebtd', h, Wd2) + bd2[:, None, None, :]
        losses = jnp.mean((recon - x[None]) ** 2, axis=(2, 3))
        idx = jnp.argmin(losses, axis=0)
        a = jax.nn.relu(jnp.einsum('btd,bdr->btr', x, Wa_down[idx]) + ba_down[idx][:, None, :])
        adapter_out = jnp.einsum('btr,bro->bto', a, Wa_up[idx]) + ba_up[idx][:, None, :]
        return base + adapter_out

    def _L1_attn_ref(x, conv_kernel, A_log, W_bc, b_bc, Dcoeff, W_dt, b_dt, W_dtp, b_dtp):
        import jax, jax.numpy as jnp
        import numpy as np
        from jax import lax
        B, L, D, N, DT_RANK = (2, 256, 128, 16, 64)

        def _scan_op(l, r):
            g_l, h_l = l
            g_r, h_r = r
            return (g_l * g_r, g_r * h_l + h_r)
        u = lax.conv_general_dilated(x, conv_kernel, window_strides=(1,), padding='SAME', dimension_numbers=('NWC', 'WIO', 'NWC'), feature_group_count=D)
        u = jax.nn.silu(u)
        Acoeff = -jnp.exp(A_log)
        BC = u @ W_bc + b_bc
        Bcoeff, Ccoeff = jnp.split(BC, 2, axis=-1)
        dt = (u @ W_dt + b_dt) @ W_dtp + b_dtp
        dt = jnp.log1p(jnp.exp(dt))
        alpha = jnp.exp(jnp.einsum('dn,bld->bldn', Acoeff, dt))
        beta = jnp.einsum('bln,bld,bld->bldn', Bcoeff, x, dt)
        _, hs = lax.associative_scan(_scan_op, (alpha, beta), axis=1)
        y = jnp.einsum('bln,bldn->bld', Ccoeff, hs)
        y = y + x * Dcoeff[None, None, :]
        return y

    def _L1_ffn_ref(x, gate_w, bias, up_w, up_b, down_w, down_b, sw_up, sb_up, sw_down, sb_down):
        import jax, jax.numpy as jnp
        import numpy as np
        H = 128
        I = 4 * H
        E = 8
        K = 2
        B, S = (2, 128)
        STD = 0.02 / np.sqrt(H)
        b, s, h = x.shape
        xf = x.reshape(-1, h)
        T = xf.shape[0]
        scores = jax.nn.sigmoid(xf @ gate_w + bias)
        top_scores, top_idx = jax.lax.top_k(scores, K)
        top_scores = top_scores / (jnp.sum(top_scores, axis=-1, keepdims=True) + 1e-06)
        w = jnp.zeros((T, E), dtype=xf.dtype).at[jnp.arange(T)[:, None], top_idx].add(top_scores)
        up = jnp.einsum('th,ehi->tei', xf, up_w) + up_b
        hact = jax.nn.gelu(up, approximate=False)
        eo = jnp.einsum('tei,eih->teh', hact, down_w) + down_b
        combined = jnp.einsum('teh,te->th', eo * 0.1, w)
        shared = (jax.nn.gelu(xf @ sw_up + sb_up, approximate=False) @ sw_down + sb_down) * 0.1
        out = (shared + combined).reshape(b, s, h)
        out = out / (jnp.max(jnp.abs(out), axis=-1, keepdims=True) + 1e-06)
        return out
    x = L0_attn_x
    x = x + 0.5 * _L0_ffn_ref(_layernorm(x, axis=-1), L0_ffn_W_base, L0_ffn_b_base, L0_ffn_Wd1, L0_ffn_bd1, L0_ffn_Wd2, L0_ffn_bd2, L0_ffn_Wa_down, L0_ffn_ba_down, L0_ffn_Wa_up, L0_ffn_ba_up)
    x = x + _L0_attn_ref(_layernorm(x, axis=-1), L0_attn_qkv_weight, L0_attn_qkv_weight_mask, L0_attn_out_weight, L0_attn_out_weight_mask, L0_attn_out_bias, L0_attn_out_bias_mask)
    x = x + 0.5 * _L0_ffn_ref(_layernorm(x, axis=-1), L0_ffn_W_base, L0_ffn_b_base, L0_ffn_Wd1, L0_ffn_bd1, L0_ffn_Wd2, L0_ffn_bd2, L0_ffn_Wa_down, L0_ffn_ba_down, L0_ffn_Wa_up, L0_ffn_ba_up)
    x = x + 0.5 * _L1_ffn_ref(_layernorm(x, axis=-1), L1_ffn_gate_w, L1_ffn_bias, L1_ffn_up_w, L1_ffn_up_b, L1_ffn_down_w, L1_ffn_down_b, L1_ffn_sw_up, L1_ffn_sb_up, L1_ffn_sw_down, L1_ffn_sb_down)
    x = x + _L1_attn_ref(_layernorm(x, axis=-1), L1_attn_conv_kernel, L1_attn_A_log, L1_attn_W_bc, L1_attn_b_bc, L1_attn_Dcoeff, L1_attn_W_dt, L1_attn_b_dt, L1_attn_W_dtp, L1_attn_b_dtp)
    x = x + 0.5 * _L1_ffn_ref(_layernorm(x, axis=-1), L1_ffn_gate_w, L1_ffn_bias, L1_ffn_up_w, L1_ffn_up_b, L1_ffn_down_w, L1_ffn_down_b, L1_ffn_sw_up, L1_ffn_sb_up, L1_ffn_sw_down, L1_ffn_sb_down)
    return x

_drawn_inputs = setup_inputs


def setup_inputs(seed=0):
    import zlib

    import numpy as np

    out = dict(_drawn_inputs(seed))
    spreads = {'L0_ffn_b_base': (0.0, 0.1),
     'L0_ffn_bd1': (0.0, 0.1),
     'L0_ffn_bd2': (0.0, 0.1),
     'L0_ffn_ba_down': (0.0, 0.1),
     'L0_ffn_ba_up': (0.0, 0.1),
     'L1_attn_b_bc': (0.0, 0.322),
     'L1_attn_Dcoeff': (1.0, 0.2),
     'L1_attn_b_dt': (0.0, 0.8),
     'L1_ffn_bias': (0.0, 0.1),
     'L1_ffn_up_b': (0.0, 0.8),
     'L1_ffn_down_b': (0.0, 0.1),
     'L1_ffn_sb_up': (0.0, 0.8),
     'L1_ffn_sb_down': (0.0, 0.1)}
    factors = {'L1_ffn_up_w': 25.652, 'L1_ffn_down_w': 8.0, 'L1_ffn_sw_up': 8.0, 'L1_ffn_sw_down': 8.0}
    for name, (base, spread) in spreads.items():
        noise = np.random.default_rng([zlib.crc32(name.encode()), seed]).standard_normal(out[name].shape)
        drawn = base * np.exp(spread * noise) if base else spread * noise
        out[name] = jnp.asarray(drawn.astype(out[name].dtype))
    for name, factor in factors.items():
        out[name] = (out[name] * factor).astype(out[name].dtype)
    return out
```

```python
from collections import namedtuple
from contextlib import ExitStack

import concourse.bass as bass
from concourse import mybir

ALU = mybir.AluOpType
ACT = mybir.ActivationFunctionType
AX = mybir.AxisListType
F32 = mybir.dt.float32
BF16 = mybir.dt.bfloat16

P = 128
NB, L, D = 8, 512, 128
NC = L // P
EPS = 1e-5


def record(**named):
    return namedtuple("Record", named)(**named)


def over_sequences(eng, step):
    step(0, None, 0)
    with eng.Fori(0, NB // 2 - 1) as i:
        step(2 * i + 1, 2 * i, 1)
        step(2 * i + 2, 2 * i + 1, 0)
    step(NB - 1, NB - 2, 1)
    step(None, NB - 1, 0)


class Chain:

    def __init__(self, eng, sem, per):
        self.eng, self.sem, self.per = eng, sem, per

    def begin(self, b):
        self.at, self.n = b * self.per, 0

    def link(self, ins):
        self.n += 1
        ins.then_inc(self.sem, 1)
        self.eng.wait_ge(self.sem, self.at + self.n)

    def end(self):
        assert self.n == self.per, (self.n, self.per)



def set_up(nc, g, ins, sem):
    x_in = [sem(f"x{b}_in") for b in range(NB)]
    made = sem("consts_made")
    with nc.Block() as block:
        @block.sync
        def _(sp):
            for b in range(NB):
                sp.dma_start(g.X[:, b], ins["L0_attn_x"][b].rearrange("(c p) d -> p c d", p=P)).then_inc(x_in[b], 16)

        @block.gpsimd
        def _(pool):
            pool.memset(g.identf[:, :], 0.0).then_inc(made, 1)
            pool.memset(g.onesf[:, :], 1.0)
            pool.memset(g.neghalf[:, :, :], -0.5).then_inc(made, 1)
            pool.wait_ge(made, 2)
            pool.affine_select(out=g.identf[:, :], in_=g.identf[:, :], compare_op=ALU.not_equal, fill=1.0,
                               base=0, pattern=[[-1, P]], channel_multiplier=1).then_inc(made, 1)

        @block.vector
        def _(dve):
            for b in range(NB):
                take_stats(dve, g, b, x_in[b], 16)


def take_stats(dve, g, b, x_done, n):
    dve.wait_ge(x_done, n)
    dve.tensor_scalar(g.carrier[:, b, :], g.X[:, b, 0, 0:1], 1.0, None, ALU.mult)
    for c in range(NC):
        last = dve.bn_stats(g.bn6[:, b, c, :], g.X[:, b, c, :])
    return last


def take_variance(dve, g, step):
    even, odd = (lambda k: g.bn6[:, :, :, k]), (lambda k: g.bn6[:, :, :, 3 + k])
    t, u = g.ln_t, g.ln_u
    dve.tensor_tensor(g.mean[:, :, :], even(1), odd(1), ALU.add)
    dve.tensor_tensor(t[:, :, :], even(1), odd(1), ALU.subtract)
    dve.tensor_tensor(u[:, :, :], even(2), odd(2), ALU.add).then_inc(step, 1)
    dve.wait_ge(step, 1)
    dve.scalar_tensor_tensor(out=t[:, :, :], in0=t[:, :, :], scalar=0.25, in1=t[:, :, :], op0=ALU.mult, op1=ALU.mult)
    dve.tensor_scalar(u[:, :, :], u[:, :, :], 1.0 / D, EPS, ALU.mult, ALU.add)
    dve.tensor_scalar(g.mean[:, :, :], g.mean[:, :, :], 0.5, None, ALU.mult).then_inc(step, 1)
    dve.wait_ge(step, 2)
    dve.tensor_tensor(u[:, :, :], u[:, :, :], t[:, :, :], ALU.add).then_inc(step, 1)


def take_rstd(pool, g, step, ready):
    pool.wait_ge(step, 3)
    for b in range(NB):
        pool.tensor_tensor(g.rstd[:, b, :], g.ln_u[:, b, :], g.neghalf[:, b, :], ALU.pow).then_inc(ready, 1)


def normalise(dve, g, b, out, rstd_ready):
    dve.wait_ge(rstd_ready, b + 1)
    for c in range(NC):
        last = dve.tensor_scalar(out[:, c, :], g.X[:, b, c, :], g.mean[:, b, c:c + 1], g.rstd[:, b, c:c + 1],
                                 ALU.subtract, ALU.mult)
    return last



E0, H0, R0 = 8, 32, 64
HALF = E0 // 2
WSEL = R0 + D + 1
LOSSCOL = P + D + 1


def adapter_weights(nc, g, w, ins, sem):
    ld = sem("aw_loaded")
    ld2 = sem("aw_bias_loaded")
    mk = sem("aw_masks")
    tr = sem("aw_transposed")
    cp = sem("aw_copied")
    mm = sem("aw_products")
    st = sem("aw_steps")
    with ExitStack() as ctx:
        w2 = ctx.enter_context(nc.sbuf_tensor("aw_w2", [P, 2, D], F32))
        w2T = ctx.enter_context(nc.sbuf_tensor("aw_w2T", [P, 2, P], F32))
        block_mask = ctx.enter_context(nc.sbuf_tensor("aw_block", [P, HALF, H0], F32))
        base_row = ctx.enter_context(nc.sbuf_tensor("aw_base", [1, D], F32))
        base_at = ctx.enter_context(nc.sbuf_tensor("aw_base_at", [R0 + 1, D], F32))
        junk = ctx.enter_context(nc.sbuf_tensor("aw_junk", [P, E0], F32))
        pT = ctx.enter_context(nc.psum_tensor("aw_pT", [P, 2, 512], F32))
        pW = ctx.enter_context(nc.psum_tensor("aw_pW", [P, 2, 512], F32))
        pB = ctx.enter_context(nc.psum_tensor("aw_pB", [P, 2, 512], F32))
        block = ctx.enter_context(nc.Block())

        @block.sync
        def _(sp):
            sp.dma_start(w2[:, :, :], ins["L0_ffn_Wd2"].rearrange("(g e) h d -> (e h) g d", g=2)).then_inc(ld, 16)
            sp.dma_start(w.wd1[:, :, :], ins["L0_ffn_Wd1"].rearrange("e d h -> d e h")).then_inc(ld, 16)
            sp.dma_start(w.sel[:, :, 0:R0], ins["L0_ffn_Wa_down"].rearrange("e d r -> d e r")).then_inc(ld, 16)
            sp.dma_start(w.wbase[:, :], ins["L0_ffn_W_base"]).then_inc(ld, 16)

        @block.scalar
        def _(act):
            act.wait_ge(mk, 1)
            act.dma_start(w.sel[0:R0, :, R0:R0 + D], ins["L0_ffn_Wa_up"].rearrange("e r o -> r e o")).then_inc(ld2, 16)
            act.dma_start(w.sel[R0:R0 + 1, :, R0:R0 + D], ins["L0_ffn_ba_up"].rearrange("(a e) o -> a e o", a=1)
                          ).then_inc(ld2, 16)
            act.dma_start(w.sel[0:R0, :, R0 + D], ins["L0_ffn_ba_down"].rearrange("e r -> r e"),
                          allow_slow_non_contiguous=True).then_inc(ld2, 16)
            act.dma_start(w.bd1[:, :], ins["L0_ffn_bd1"].rearrange("(a e) h -> a (e h)", a=1)).then_inc(ld2, 16)
            act.dma_start(w.b2T[:, :], ins["L0_ffn_bd2"].rearrange("e d -> d e"),
                          allow_slow_non_contiguous=True).then_inc(ld2, 16)
            act.dma_start(base_at[R0:R0 + 1, :], ins["L0_ffn_b_base"].rearrange("(a o) -> a o", a=1)).then_inc(ld2, 16)

        @block.gpsimd
        def _(pool):
            pool.memset(w.sel[:, :, R0:WSEL], 0.0).then_inc(mk, 1)
            pool.memset(block_mask[:, :, :], 1.0)
            pool.memset(w.expert_mask[:, :, :], 0.0).then_inc(mk, 1)
            pool.wait_ge(mk, 2)
            pool.affine_select(out=block_mask[:, :, :], in_=block_mask[:, :, :], compare_op=ALU.is_ge, fill=0.0,
                               base=0, pattern=[[-H0, HALF], [0, H0]], channel_multiplier=1).then_inc(mk, 1)
            pool.wait_ge(mk, 3)
            pool.affine_select(out=block_mask[:, :, :], in_=block_mask[:, :, :], compare_op=ALU.is_ge, fill=0.0,
                               base=H0 - 1, pattern=[[H0, HALF], [0, H0]], channel_multiplier=-1).then_inc(mk, 1)
            pool.wait_ge(mk, 4)
            for half in range(2):
                last = pool.tensor_copy(w.expert_mask[:, half, half * HALF:(half + 1) * HALF], block_mask[:, :, 0])
            last.then_inc(mk, 1)
            pool.iota(w.down_count[:, :], pattern=[[1, E0]], base=-E0, channel_multiplier=0,
                      allow_small_or_imprecise_dtypes=True).then_inc(mk, 1)

        @block.tensor
        def _(pe):
            pe.wait_ge(ld, 64)
            for half in range(2):
                last = pe.transpose(pT[:, half, 0:P], w2[:, half, :], g.identf[:, :])
            last.then_inc(tr, 1)
            pe.wait_ge(cp, 1)
            pe.wait_ge(ld2, 96)
            for half in range(2):
                pe.matmul(pW[:, half, 0:P], w2T[:, half, :], w2T[:, half, :], start=True, stop=True)
                last = pe.matmul(pB[:, half, 0:E0], w2T[:, half, :], w.b2T[:, :], start=True, stop=True)
            last.then_inc(mm, 1)

        @block.vector
        def _(dve):
            dve.wait_ge(ld, 64)
            dve.wait_ge(ld2, 96)
            dve.wait_ge(mk, 6)
            dve.tensor_tensor(w.sel[R0:R0 + 1, :, R0:R0 + D], w.sel[R0:R0 + 1, :, R0:R0 + D],
                              base_at[R0:R0 + 1, :].rearrange("p (a o) -> p a o", a=1).broadcast_to([1, E0, D]), ALU.add)
            dve.wait_ge(tr, 1)
            dve.tensor_copy(w2T[:, :, :], pT[:, :, 0:P]).then_inc(cp, 1)
            for half in range(2):
                x_cols = slice(P, P + D) if half == 0 else slice(0, D)
                dve.tensor_scalar(w.loss[:, half, x_cols], w2[:, half, :], -2.0, None, ALU.mult)
            dve.tensor_scalar(w.b2_slope[:, :], w.b2T[:, :], -2.0, None, ALU.mult)
            dve.scalar_tensor_tensor(out=w.b2_const[:, :], in0=w.b2T[:, :], scalar=float(L), in1=w.b2T[:, :],
                                     op0=ALU.mult, op1=ALU.mult)
            dve.wait_ge(mm, 1)
            for half in range(2):
                h_cols = slice(0, P) if half == 0 else slice(D + 1, LOSSCOL)
                one = P + D if half == 0 else D
                dve.tensor_tensor(w.loss[:, half, h_cols], pW[:, half, 0:P],
                                  block_mask[:, :, :].rearrange("p e h -> p (e h)"), ALU.mult)
                dve.tensor_tensor_reduce(junk[:, :], pB[:, half, 0:E0], w.expert_mask[:, half, :], 2.0, 0.0,
                                         ALU.mult, ALU.add, w.loss[:, half, one:one + 1]).then_inc(st, 1)
                dve.wait_ge(st, half + 1)


def adapter_ffn(nc, g, w, sem, tag):
    s = record(**{n: sem(f"{tag}_{n}") for n in (
        "var", "rstd", "ones", "xn_ready", "xT_done", "xT_ready", "h_done", "h_ready", "gram_done", "score_ready", "loss_done",
        "adapter_ready", "a_done", "a_ready", "y_done", "y_free", "pick", "score")})
    with ExitStack() as ctx:
        def sb(name, shape):
            return ctx.enter_context(nc.sbuf_tensor(f"{tag}_{name}", shape, F32))

        def ps(name, shape):
            return ctx.enter_context(nc.psum_tensor(f"{tag}_{name}", shape, F32))

        hx = [sb(f"hx{i}", [P, NC, 2 * P + D + 1]) for i in range(2)]
        xT = [sb(f"xT{i}", [P, L]) for i in range(2)]
        picked = [sb(f"picked{i}", [P, WSEL]) for i in range(2)]
        aT = [sb(f"aT{i}", [R0 + 1, L]) for i in range(2)]
        junk = sb("junk", [P, 2, LOSSCOL])
        part = sb("part", [P, 2])
        score = sb("score", [P, E0])
        small = sb("small", [P, 4, E0])
        pT = ps("pT", [P, NC, P])
        pH = [ps(f"pH{i}", [P, 2, 2 * P]) for i in range(2)]
        pG = [ps(f"pG{i}", [P, 512]) for i in range(2)]
        pS = ps("pS", [P, 512])
        pA = ps("pA", [P, 512])
        pY = ps("pY", [P, NC, D])
        x_cols = slice(P, P + D)
        one_col = slice(P + D, P + D + 1)
        gram_cols = [slice(0, LOSSCOL), slice(P, P + LOSSCOL)]
        h_cols = [slice(0, P), slice(P + D + 1, 2 * P + D + 1)]
        block = ctx.enter_context(nc.Block())

        @block.gpsimd
        def _(pool):
            take_rstd(pool, g, s.var, s.rstd)
            for i in range(2):
                pool.memset(hx[i][:, :, one_col], 1.0)
                last = pool.memset(aT[i][:, :], 1.0)
            last.then_inc(s.ones, 1)

        @block.tensor
        def _(pe):
            pe.wait_ge(s.ones, 1)

            def step(new, old, par):
                if new is not None:
                    pe.wait_ge(s.xn_ready, new + 1)
                    for c in range(NC):
                        last = pe.transpose(pT[:, c, :], hx[par][:, c, x_cols], g.identf[:, :])
                    last.then_inc(s.xT_done, 1)
                    pe.wait_ge(s.xT_ready, new + 1)
                    for c in range(NC):
                        pe.matmul(pH[c // 2][:, c % 2, :], g.onesf[0:1, :], w.bd1[:, :], start=True, stop=False)
                        last = pe.matmul(pH[c // 2][:, c % 2, :], xT[par][:, c * P:(c + 1) * P],
                                         w.wd1[:, :, :].rearrange("d e h -> d (e h)"), start=False, stop=True)
                        if c % 2:
                            last.then_inc(s.h_done, 1)
                if old is not None:
                    pe.wait_ge(s.adapter_ready, old + 1)
                    pe.matmul(pA[0:R0, :], picked[1 - par][:, 0:R0], xT[1 - par][:, :],
                              start=True, stop=True).then_inc(s.a_done, 1)
                if new is not None:
                    pe.wait_ge(s.h_ready, 2 * new + 2)
                    for half in range(2):
                        for c in range(NC):
                            pe.matmul(pG[half][:, 0:LOSSCOL], hx[par][:, c, h_cols[half]],
                                      hx[par][:, c, gram_cols[half]], start=(c == 0), stop=(c == NC - 1))
                    for c in range(NC):
                        last = pe.matmul(pS[:, 0:1], hx[par][:, c, x_cols], hx[par][:, c, one_col],
                                         start=(c == 0), stop=(c == NC - 1))
                    last.then_inc(s.gram_done, 1)
                if old is not None:
                    pe.wait_ge(s.a_ready, old + 1)
                    pe.wait_ge(s.y_free, old + 1)
                    for c in range(NC):
                        pe.matmul(pY[:, c, :], xT[1 - par][:, c * P:(c + 1) * P], w.wbase[:, :],
                                  start=True, stop=False)
                        last = pe.matmul(pY[:, c, :], aT[1 - par][:, c * P:(c + 1) * P],
                                         picked[1 - par][0:R0 + 1, R0:R0 + D], start=False, stop=True)
                    last.then_inc(s.y_done, 1)
                if new is not None:
                    pe.wait_ge(s.score_ready, new + 1)
                    pe.matmul(pS[:, E0:2 * E0], g.onesf[:, :], score[:, :], start=True, stop=True
                              ).then_inc(s.loss_done, 1)

            over_sequences(pe, step)

        @block.scalar
        def _(act):
            def step(new, old, par):
                if new is not None:
                    act.wait_ge(s.xT_done, new + 1)
                    act.copy(xT[par][:, :], pT[:, :, :].rearrange("p c t -> p (c t)")).then_inc(s.xT_ready, 1)
                    for q in range(2):
                        act.wait_ge(s.h_done, 2 * new + q + 1)
                        for half in range(2):
                            last = act.activation(hx[par][:, 2 * q:2 * q + 2, h_cols[half]],
                                                  pH[q][:, :, half * P:(half + 1) * P], ACT.Relu)
                        last.then_inc(s.h_ready, 1)
                if old is not None:
                    act.wait_ge(s.a_done, old + 1)
                    act.activation(aT[1 - par][0:R0, :], pA[0:R0, :], ACT.Relu,
                                   bias=picked[1 - par][0:R0, R0 + D:WSEL]).then_inc(s.a_ready, 1)

            over_sequences(act, step)

        @block.vector
        def _(dve):
            score_chain = Chain(dve, s.score, 3)
            pick_chain = Chain(dve, s.pick, 3 + E0 - 1)

            def norm(b, par):
                normalise(dve, g, b, hx[par][:, :, x_cols], s.rstd).then_inc(s.xn_ready, 1)

            def step(new, old, par):
                if new is not None:
                    if not isinstance(new, int) or new < NB - 1:
                        norm(new + 1, 1 - par)
                    dve.wait_ge(s.gram_done, new + 1)
                    score_chain.begin(new)
                    for half in range(2):
                        dve.tensor_tensor_reduce(junk[:, half, :], pG[half][:, 0:LOSSCOL], w.loss[:, half, :], 1.0,
                                                 0.0, ALU.mult, ALU.add, part[:, half:half + 1])
                    score_chain.link(dve.scalar_tensor_tensor(out=score[:, :], in0=w.b2_slope[:, :],
                                                              scalar=pS[:, 0:1], in1=w.b2_const[:, :],
                                                              op0=ALU.mult, op1=ALU.add))
                    score_chain.link(dve.scalar_tensor_tensor(out=score[:, :], in0=w.expert_mask[:, 0, :],
                                                              scalar=part[:, 0:1], in1=score[:, :],
                                                              op0=ALU.mult, op1=ALU.add))
                    dve.scalar_tensor_tensor(out=score[:, :], in0=w.expert_mask[:, 1, :], scalar=part[:, 1:2],
                                             in1=score[:, :], op0=ALU.mult, op1=ALU.add).then_inc(s.score_ready, 1)
                    dve.wait_ge(s.loss_done, new + 1)
                    pick_chain.begin(new)
                    loss = pS[:, E0:2 * E0]
                    score_chain.link(dve.tensor_reduce(small[:, 0, 0:1], loss, AX.X, ALU.min))
                    score_chain.end()
                    pick_chain.link(dve.scalar_tensor_tensor(out=small[:, 1, :], in0=loss, scalar=small[:, 0, 0:1],
                                                             in1=w.down_count[:, :], op0=ALU.is_equal, op1=ALU.mult))
                    pick_chain.link(dve.tensor_reduce(small[:, 0, 1:2], small[:, 1, :], AX.X, ALU.min))
                    pick_chain.link(dve.tensor_scalar(small[:, 2, :], w.down_count[:, :], small[:, 0, 1:2], None,
                                                      ALU.is_equal))
                    out = picked[par][:, :]
                    for e in range(E0):
                        if e == 0:
                            ins = dve.tensor_scalar(out, w.sel[:, e, :], small[:, 2, e:e + 1], None, ALU.mult)
                        else:
                            ins = dve.scalar_tensor_tensor(out=out, in0=w.sel[:, e, :], scalar=small[:, 2, e:e + 1],
                                                           in1=out, op0=ALU.mult, op1=ALU.add)
                        if e < E0 - 1:
                            pick_chain.link(ins)
                    pick_chain.end()
                    ins.then_inc(s.adapter_ready, 1)
                if old is not None:
                    dve.wait_ge(s.y_done, old + 1)
                    x = g.X[:, old]
                    dve.scalar_tensor_tensor(out=x, in0=pY[:, :, :], scalar=0.5, in1=x, op0=ALU.mult, op1=ALU.add
                                             ).then_inc(s.y_free, 1)
                    take_stats(dve, g, old, s.y_free, old + 2)

            dve.sem_inc(s.y_free, 1)
            take_variance(dve, g, s.var)
            dve.wait_ge(s.ones, 1)
            norm(0, 0)
            over_sequences(dve, step)



NH, DH = 16, D // 16
GROUPS, GH = 4, 4
PAIRS = NH // 2
SCALE = float(D) ** -0.5
Q_PARTS = (0, 0, 0, 1, 1, 2)
K_PARTS = (0, 1, 2, 0, 1, 0)
STACK = len(Q_PARTS) * DH
LOAD_COUNT = 16 * 4
VW = 32


def attention_weights(nc, g, w, ins, sem):
    ld = sem("tw_loaded")
    mk = sem("tw_masked")
    tr = sem("tw_transposed")
    cp = sem("tw_copied")
    with ExitStack() as ctx:
        def sb(name, shape):
            return ctx.enter_context(nc.sbuf_tensor(name, shape, F32))

        wt, mask, masked = sb("tw_w", [P, 4, D]), sb("tw_m", [P, 4, D]), sb("tw_masked_w", [P, 4, D])
        bias, bias_mask = sb("tw_b", [1, D]), sb("tw_bm", [1, D])
        pT = ctx.enter_context(nc.psum_tensor("tw_pT", [P, 4, P], F32))
        block = ctx.enter_context(nc.Block())

        @block.sync
        def _(sp):
            for dst, qkv, out in ((wt, "L0_attn_qkv_weight", "L0_attn_out_weight"),
                                  (mask, "L0_attn_qkv_weight_mask", "L0_attn_out_weight_mask")):
                sp.dma_start(dst[:, 0:3, :], ins[qkv].rearrange("(j o) k -> o j k", o=P)).then_inc(ld, 16)
                sp.dma_start(dst[:, 3, :], ins[out]).then_inc(ld, 16)
            sp.dma_start(bias[:, :], ins["L0_attn_out_bias"].rearrange("(a o) -> a o", a=1)).then_inc(ld, 16)
            sp.dma_start(bias_mask[:, :], ins["L0_attn_out_bias_mask"].rearrange("(a o) -> a o", a=1)).then_inc(ld, 16)

        @block.vector
        def _(dve):
            dve.wait_ge(ld, 96)
            dve.scalar_tensor_tensor(out=masked[:, :, :], in0=mask[:, :, :], scalar=0.0, in1=wt[:, :, :],
                                     op0=ALU.is_gt, op1=ALU.mult).then_inc(mk, 1)
            dve.scalar_tensor_tensor(out=w.bo[:, :], in0=bias_mask[:, :], scalar=0.0, in1=bias[:, :],
                                     op0=ALU.is_gt, op1=ALU.mult)
            dve.wait_ge(tr, 1)
            dve.tensor_copy(w.wT[:, :, :], pT[:, :, :]).then_inc(cp, 1)

        @block.tensor
        def _(pe):
            pe.wait_ge(mk, 1)
            for j in range(4):
                last = pe.transpose(pT[:, j, :], masked[:, j, :], g.identf[:, :])
            last.then_inc(tr, 1)


Z_PLAN = [("max1", "seq", 0, "end"), ("xT", "next", 1, "mid"), ("out3", "prev", 1, "end"), ("q", "next", 2, "mid"),
          ("oT", "prev", 2, "end"), ("k", "next", 3, "mid"), ("y", "prev", 3, "end"), ("max2", "seq", 4, "end"),
          ("v", "next", 5, "mid"), ("out0", "seq", 5, "end"), ("max3", "seq", 8, "end"), ("out1", "seq", 9, "end"),
          ("max0", "next", 12, "end"), ("out2", "seq", 13, "end")]
Z_HEAD = ["xT", "q", "k", "v", "max0"]


def z_place(prev, seq, nxt):
    who = {"prev": prev, "seq": seq, "next": nxt}
    per = len(Z_PLAN)
    missing_first = sum(whose == "prev" for _, whose, _, _ in Z_PLAN)
    missing_last = sum(whose == "next" for _, whose, _, _ in Z_PLAN)
    if seq is None:
        at = len(Z_HEAD) + NB * per - missing_first - missing_last
    elif prev is None:
        at = len(Z_HEAD)
    else:
        at = seq * per + (len(Z_HEAD) - missing_first)
    out = {}
    for event, whose, slot, place in Z_PLAN:
        if who[whose] is not None:
            out[slot, place] = (event, who[whose], at)
            at = at + 1
    return out


def attention(nc, g, w, sem):
    s = record(**{n: sem(f"at_{n}") for n in (
        "var", "rstd", "xn_ready", "z_done", "q_high", "q_rest", "q_split", "q_out", "k_high", "k_rest", "k_split",
        "k_out", "v_ready", "va_in", "st_done", "exp_done", "pv_done", "o_free", "ao_ready", "x_done", "mx_done", "mx_free",
        "m_high", "m_rest", "m_split", "m_low", "m_out", "rden", "xT_ready", "oT_ready", "qk_low", "ones")})
    load_in = [sem(f"at_load{i}") for i in range(GROUPS)]
    m_in = [sem(f"at_m_in{i}") for i in range(GROUPS)]
    q_dram = nc.dram_tensor("q_stack", (NH, len(Q_PARTS), DH, L), BF16, kind="Internal").ap()
    k_dram = nc.dram_tensor("k_stack", (NH, len(K_PARTS), DH, L), BF16, kind="Internal").ap()
    m_dram = nc.dram_tensor("m_parts", (NH, 3, L), BF16, kind="Internal").ap()
    with ExitStack() as ctx:
        def sb(name, shape, dt=F32):
            return ctx.enter_context(nc.sbuf_tensor(f"at_{name}", shape, dt))

        def ps(name, shape):
            return ctx.enter_context(nc.psum_tensor(f"at_{name}", shape, F32))

        xn = sb("xn", [P, NC, D])
        xT = sb("xT", [P, L])
        qs, ks = sb("qs", [P, 3, L], BF16), sb("ks", [P, 3, L], BF16)
        qr, kr = sb("qr", [P, L]), sb("kr", [P, L])
        zero = sb("zero", [P, L])
        qq, kk = sb("qq", [P, PAIRS, L], BF16), sb("kk", [P, PAIRS, L], BF16)
        vt = sb("vt", [P, NC, D])
        va = sb("va", [P, NC, NH, VW])
        probs = sb("probs", [P, 2 * GH, L])
        nm = [sb(f"nm{i}", [P, NC, GH]) for i in range(2)]
        ms = sb("ms", [GH, 3, L], BF16)
        mr = sb("mr", [GH, L])
        os = sb("os", [P, L])
        rden = sb("rden", [P, NC, GH])
        ao = sb("ao", [P, NC, D])
        oT = sb("oT", [P, L])
        mx = [ps(f"mx{i}", [P, 2, L]) for i in range(2)]
        st = [ps(f"st{i}", [P, L]) for i in range(2)]
        po = ps("po", [P, L])
        z = ps("z", [P, L])
        z3 = z[:, :].rearrange("p (c d) -> p c d", c=NC)
        block = ctx.enter_context(nc.Block())

        def rows(h, n):
            return slice(64 * (h % 2), 64 * (h % 2) + n)

        def max_head(slot, seq, nxt):
            h = slot + 2 * GH
            return (seq, h) if h < NH else (nxt, h - NH)

        def over_all(eng, iteration):
            iteration(None, 0, 1)
            with eng.Fori(1, NB - 1) as b:
                iteration(b - 1, b, b + 1)
            iteration(NB - 2, NB - 1, None)
            iteration(NB - 1, None, None)

        @block.gpsimd
        def _(pool):
            take_rstd(pool, g, s.var, s.rstd)
            pool.memset(kk[:, :, :], 1.0)
            pool.memset(va[:, :, :, :], 0.0).then_inc(s.ones, 1)
            pool.memset(zero[:, :], 0.0)
            pool.wait_ge(s.ones, 1)
            pool.memset(va[:, :, :, DH:DH + 1], 1.0).then_inc(s.ones, 1)
            pool.wait_ge(s.ones, 2)

            def split(rest, parts, rest_sem, low_sem, split_sem, n):
                pool.wait_ge(rest_sem, n)
                pool.tensor_tensor(parts[:, 1, :], rest[:, :], zero[0:GH, :], ALU.add).then_inc(low_sem, 1)
                pool.wait_ge(low_sem, n)
                pool.tensor_tensor(parts[:, 2, :], rest[:, :], parts[:, 1, :], ALU.subtract).then_inc(split_sem, 1)

            def split_k(n):
                pool.wait_ge(s.k_rest, n)
                pool.tensor_tensor(ks[:, 1, :], kr[:, :], zero[:, :], ALU.add).then_inc(s.qk_low, 1)
                pool.wait_ge(s.qk_low, 2 * n)
                pool.tensor_tensor(ks[:, 2, :], kr[:, :], ks[:, 1, :], ALU.subtract).then_inc(s.k_split, 1)

            def split_q(n):
                if not isinstance(n, int) or n > 1:
                    pool.wait_ge(load_in[GROUPS - 1], LOAD_COUNT * (n - 1))
                pool.wait_ge(s.q_rest, n)
                pool.tensor_tensor(qs[:, 1, :], qr[:, :], zero[:, :], ALU.add).then_inc(s.qk_low, 1)
                pool.wait_ge(s.qk_low, 2 * n - 1)
                pool.tensor_tensor(qs[:, 2, :], qr[:, :], qs[:, 1, :], ALU.subtract).then_inc(s.q_split, 1)

            def split_max(seq, group):
                split(mr, ms, s.m_rest, s.m_low, s.m_split, seq * GROUPS + group + 1)

            def spread_values(seq, group):
                pool.wait_ge(s.v_ready, seq + 1)
                if not isinstance(seq, int) or seq > 0:
                    pool.wait_ge(s.pv_done, (seq - 1) * 16 + 4 * group + 4)
                heads = slice(group * GH, (group + 1) * GH)
                pool.tensor_tensor(
                    va[:, :, heads, 0:DH], vt[:, :, group * GH * DH:(group + 1) * GH * DH].rearrange(
                        "p c (h d) -> p c h d", h=GH),
                    zero[:, 0:NC * GH * DH].rearrange("p (c h d) -> p c h d", c=NC, h=GH), ALU.add
                ).then_inc(s.va_in, 1)

            def iteration(prev, seq, nxt):
                if seq is None:
                    return
                split_max(seq, 1)
                if prev is not None:
                    spread_values(seq, 3)
                if nxt is not None:
                    split_q(nxt + 1)
                    split_k(nxt + 1)
                split_max(seq, 2)
                if nxt is not None:
                    spread_values(nxt, 0)
                split_max(seq, 3)
                if nxt is not None:
                    spread_values(nxt, 1)
                    split_max(nxt, 0)
                    spread_values(nxt, 2)

            split_q(1)
            split_k(1)
            for group in range(GROUPS):
                spread_values(0, group)
            split_max(0, 0)
            over_all(pool, iteration)

        @block.sync
        def _(sp):
            sp.wait_ge(s.ones, 2)

            def write_stacks(seq):
                for parts, ready, dram, order, out in ((qs, s.q_split, q_dram, Q_PARTS, s.q_out),
                                                       (ks, s.k_split, k_dram, K_PARTS, s.k_out)):
                    sp.wait_ge(ready, seq + 1)
                    for row, part in enumerate(order):
                        sp.dma_start(dram[:, row], parts[:, part, :]).then_inc(out, 16)

            def load(seq, group):
                if not isinstance(seq, int) or seq > 0:
                    sp.wait_ge(s.st_done, 64 * seq + 16 * (group + 1) - 64)
                if group == 0:
                    sp.wait_ge(s.q_out, 96 * seq + 96)
                    sp.wait_ge(s.k_out, 96 * seq + 96)
                pairs = slice(group * 2, group * 2 + 2)
                for dst, dram in ((qq, q_dram), (kk, k_dram)):
                    src = dram.rearrange("(p x) s d i -> x (s d) p i", x=2)
                    for half in range(2):
                        sp.dma_start(dst[64 * half:64 * half + STACK, pairs, :], src[half, :, pairs, :]
                                     ).then_inc(load_in[group], 16)

            def add_max(seq, group):
                sp.wait_ge(s.m_split, GROUPS * seq + group + 1)
                heads = slice(group * GH, (group + 1) * GH)
                sp.dma_start(m_dram[heads], ms[:, :, :]).then_inc(s.m_out, 16)
                sp.wait_ge(s.m_out, 16 * GROUPS * seq + 16 * (group + 1))
                src = m_dram.rearrange("(p x) s i -> x s p i", x=2)
                for half in range(2):
                    sp.dma_start(qq[64 * half + STACK:64 * half + STACK + 3, 2 * group:2 * group + 2, :],
                                 src[half, :, 2 * group:2 * group + 2, :]).then_inc(m_in[group], 16)

            def iteration(prev, seq, nxt):
                if seq is None:
                    return
                if prev is not None:
                    load(seq, 3)
                add_max(seq, 1)
                if nxt is not None:
                    write_stacks(nxt)
                add_max(seq, 2)
                if nxt is not None:
                    load(nxt, 0)
                add_max(seq, 3)
                if nxt is not None:
                    load(nxt, 1)
                    add_max(nxt, 0)
                    load(nxt, 2)

            write_stacks(0)
            for group in range(GROUPS):
                load(0, group)
            add_max(0, 0)
            over_all(sp, iteration)

        @block.tensor
        def _(pe):
            def take_z(last):
                if last is not None:
                    event, seq = last
                    name, n = event.rstrip("0123"), seq + 1
                    if event != name:
                        n = seq * GROUPS + int(event[-1]) + 1
                    read = {"xT": s.xT_ready, "q": s.q_rest, "k": s.k_rest, "v": s.v_ready, "max": s.m_rest,
                            "out": s.ao_ready, "oT": s.oT_ready, "y": s.x_done}[name]
                    pe.wait_ge(read, n)

            def z_event(event, seq, before):
                if event == "xT":
                    pe.wait_ge(s.xn_ready, seq + 1)
                    take_z(before)
                    for c in range(NC):
                        last = pe.transpose(z3[:, c, :], xn[:, c, :], g.identf[:, :])
                elif event in ("q", "k"):
                    if event == "q":
                        pe.wait_ge(s.xT_ready, seq + 1)
                    take_z(before)
                    last = pe.matmul(z[:, :], w.wT[:, "qk".index(event), :], xT[:, :], start=True, stop=True)
                elif event == "v":
                    take_z(before)
                    for c in range(NC):
                        last = pe.matmul(z3[:, c, :], xT[:, c * P:(c + 1) * P], w.wT[:, 2, :], start=True, stop=True)
                elif event.startswith("max"):
                    group = int(event[3])
                    pe.wait_ge(s.mx_free, seq * 32 + 8 * (group + 1))
                    take_z(before)
                    for c in range(NC):
                        last = pe.transpose(z3[0:GH, c, :], nm[group % 2][:, c, :], g.identf[:, :])
                elif event.startswith("out"):
                    pe.wait_ge(s.o_free, seq * GROUPS + int(event[3]) + 1)
                    take_z(before)
                    for c in range(NC):
                        last = pe.transpose(z3[:, c, :], os[:, c * P:(c + 1) * P], g.identf[:, :])
                elif event == "oT":
                    take_z(before)
                    for c in range(NC):
                        last = pe.transpose(z3[:, c, :], ao[:, c, :], g.identf[:, :])
                elif event == "y":
                    pe.wait_ge(s.oT_ready, seq + 1)
                    take_z(before)
                    for c in range(NC):
                        pe.matmul(z3[:, c, :], g.onesf[0:1, :], w.bo[:, :], start=True, stop=False)
                        last = pe.matmul(z3[:, c, :], oT[:, c * P:(c + 1) * P], w.wT[:, 3, :], start=False, stop=True)
                last.then_inc(s.z_done, 1)

            def max_scores(seq, h, half):
                n = 32 * seq + 2 * h + half
                if h % GH == 0 and half == 0:
                    pe.wait_ge(load_in[h // GH], LOAD_COUNT * (seq + 1))
                if not isinstance(n, int) or n > 1:
                    pe.wait_ge(s.mx_free, n - 1)
                for c in range(2):
                    q_at = (2 * half + c) * P
                    last = pe.matmul(mx[half][:, c, :], qq[rows(h, STACK), h // 2, q_at:q_at + P],
                                     kk[rows(h, STACK), h // 2, :], start=True, stop=True)
                last.then_inc(s.mx_done, 1)

            def scores(seq, slot, h4):
                group, tile = slot // 4, slot % 4
                h = group * GH + h4
                n = 64 * seq + 4 * slot + h4
                if tile == 0 and h4 == 0:
                    pe.wait_ge(m_in[group], 32 * (seq + 1))
                if not isinstance(n, int) or n > 1:
                    pe.wait_ge(s.exp_done, n - 1)
                pe.matmul(st[h4 % 2][:, :], kk[rows(h, STACK + 3), h // 2, tile * P:(tile + 1) * P],
                          qq[rows(h, STACK + 3), h // 2, :], start=True, stop=True).then_inc(s.st_done, 1)

            def values(seq, slot):
                group, tile = slot // 4, slot % 4
                pe.wait_ge(s.exp_done, 64 * seq + 4 * slot + 4)
                if tile == 0:
                    pe.wait_ge(s.va_in, GROUPS * seq + group + 1)
                    if not (isinstance(seq, int) and seq == 0 and group == 0):
                        pe.wait_ge(s.o_free, GROUPS * seq + group)
                for h4 in range(GH):
                    last = pe.matmul(po[VW * h4:VW * (h4 + 1), :], va[:, tile, group * GH + h4, :],
                                     probs[:, (slot % 2) * GH + h4, :], start=(tile == 0), stop=(tile == 3),
                                     skip_group_check=True)
                last.then_inc(s.pv_done, 1)

            def iteration(prev, seq, nxt):
                places = z_place(prev, seq, nxt)
                last = ("max0", 0) if prev is None else ("out2", prev)
                for slot in range(16):
                    m_seq, m_h = max_head(slot, seq, nxt)
                    if m_seq is not None:
                        max_scores(m_seq, m_h, 0)
                    if seq is not None:
                        scores(seq, slot, 0)
                        scores(seq, slot, 1)
                    if (slot, "mid") in places:
                        z_event(*places[slot, "mid"][:2], last)
                        last = places[slot, "mid"][:2]
                    if m_seq is not None:
                        max_scores(m_seq, m_h, 1)
                    if seq is not None:
                        scores(seq, slot, 2)
                        scores(seq, slot, 3)
                    if slot > 0 and seq is not None:
                        values(seq, slot - 1)
                    elif slot == 0 and prev is not None:
                        values(prev, 15)
                    if (slot, "end") in places:
                        z_event(*places[slot, "end"][:2], last)
                        last = places[slot, "end"][:2]

            pe.wait_ge(s.ones, 2)
            for before, event in enumerate(Z_HEAD):
                if event == "max0":
                    for h in range(2 * GH):
                        for half in range(2):
                            max_scores(0, h, half)
                z_event(event, 0, (Z_HEAD[before - 1], 0) if before else None)
            over_all(pe, iteration)

        @block.scalar
        def _(act):
            def z_event(event, seq, before):
                if event == "xT":
                    act.wait_ge(s.z_done, before + 1)
                    act.copy(xT[:, :], z[:, :]).then_inc(s.xT_ready, 1)
                elif event in ("q", "k"):
                    parts, out, high = (qs, s.q_out, s.q_high) if event == "q" else (ks, s.k_out, s.k_high)
                    if not isinstance(seq, int) or seq > 0:
                        act.wait_ge(out, 96 * seq)
                    act.wait_ge(s.z_done, before + 1)
                    act.copy(parts[:, 0, :], z[:, :]).then_inc(high, 1)
                elif event == "v":
                    if not isinstance(seq, int) or seq > 0:
                        act.wait_ge(s.va_in, GROUPS * seq)
                    act.wait_ge(s.z_done, before + 1)
                    act.copy(vt[:, :, :], z3).then_inc(s.v_ready, 1)
                elif event.startswith("max"):
                    n = seq * GROUPS + int(event[3])
                    if not isinstance(n, int) or n > 0:
                        act.wait_ge(s.m_out, 16 * n)
                    act.wait_ge(s.z_done, before + 1)
                    act.copy(ms[:, 0, :], z[0:GH, :]).then_inc(s.m_high, 1)
                elif event == "oT":
                    act.wait_ge(s.z_done, before + 1)
                    act.copy(oT[:, :], z[:, :]).then_inc(s.oT_ready, 1)

            def take_output(seq, group):
                act.wait_ge(s.pv_done, 16 * seq + 4 * group + 4)
                act.copy(os[:, :], po[:, :]).then_inc(s.o_free, 1)

            def exponentials(seq, slot, h4):
                act.wait_ge(s.st_done, 64 * seq + 4 * slot + h4 + 1)
                act.activation(probs[:, (slot % 2) * GH + h4, :], st[h4 % 2][:, :], ACT.Exp, scale=SCALE
                               ).then_inc(s.exp_done, 1)

            def iteration(prev, seq, nxt):
                places = z_place(prev, seq, nxt)
                for slot in range(16):
                    if seq is not None:
                        exponentials(seq, slot, 0)
                        exponentials(seq, slot, 1)
                    if (slot, "mid") in places:
                        z_event(*places[slot, "mid"])
                    if seq is not None:
                        exponentials(seq, slot, 2)
                        exponentials(seq, slot, 3)
                    if slot == 0 and prev is not None:
                        take_output(prev, 3)
                    if slot % 4 == 0 and slot > 0 and seq is not None:
                        take_output(seq, slot // 4 - 1)
                    if (slot, "end") in places:
                        z_event(*places[slot, "end"])

            for before, event in enumerate(Z_HEAD):
                z_event(event, 0, before)
            over_all(act, iteration)

        @block.vector
        def _(dve):
            def z_event(event, seq, before):
                if event in ("q", "k"):
                    parts, rest, high, ready = ((qs, qr, s.q_high, s.q_rest) if event == "q" else
                                                (ks, kr, s.k_high, s.k_rest))
                    dve.wait_ge(high, seq + 1)
                    if not isinstance(seq, int) or seq > 0:
                        dve.wait_ge(s.q_split if event == "q" else s.k_split, seq)
                    dve.tensor_tensor(rest[:, :], z[:, :], parts[:, 0, :], ALU.subtract).then_inc(ready, 1)
                elif event.startswith("max"):
                    n = seq * GROUPS + int(event[3])
                    dve.wait_ge(s.m_high, n + 1)
                    if not isinstance(n, int) or n > 0:
                        dve.wait_ge(s.m_split, n)
                    dve.tensor_tensor(mr[:, :], z[0:GH, :], ms[:, 0, :], ALU.subtract).then_inc(s.m_rest, 1)
                elif event.startswith("out"):
                    group = int(event[3])
                    n = seq * GROUPS + group
                    dve.wait_ge(s.z_done, before + 1)
                    out4 = z[:, :].rearrange("p (c h v) -> p c h v", c=NC, h=GH)
                    dve.reciprocal(rden[:, :, :], out4[:, :, :, DH]).then_inc(s.rden, 1)
                    dve.wait_ge(s.rden, n + 1)
                    dve.tensor_tensor(
                        ao[:, :, group * GH * DH:(group + 1) * GH * DH].rearrange("p c (h d) -> p c h d", h=GH),
                        out4[:, :, :, 0:DH], rden[:, :, :].unsqueeze(3).broadcast_to([P, NC, GH, DH]), ALU.mult
                    ).then_inc(s.ao_ready, 1)
                elif event == "y":
                    dve.wait_ge(s.z_done, before + 1)
                    x = g.X[:, seq]
                    dve.tensor_tensor(x, z3, x, ALU.add).then_inc(s.x_done, 1)

            def row_max(seq, h, half):
                n = 32 * seq + 2 * h + half
                dve.wait_ge(s.mx_done, n + 1)
                dve.tensor_reduce(nm[(h // GH) % 2][:, 2 * half:2 * half + 2, h % GH], mx[half][:, :, :], AX.X,
                                  ALU.max, negate=True).then_inc(s.mx_free, 1)

            def iteration(prev, seq, nxt):
                places = z_place(prev, seq, nxt)
                for slot in range(16):
                    m_seq, m_h = max_head(slot, seq, nxt)
                    if m_seq is not None:
                        row_max(m_seq, m_h, 0)
                    if (slot, "mid") in places:
                        z_event(*places[slot, "mid"])
                    if m_seq is not None:
                        row_max(m_seq, m_h, 1)
                    if slot == 0 and nxt is not None:
                        normalise(dve, g, nxt, xn[:, :, :], s.rstd).then_inc(s.xn_ready, 1)
                    if (slot, "end") in places:
                        z_event(*places[slot, "end"])
                    if slot == 4 and prev is not None:
                        take_stats(dve, g, prev, s.x_done, prev + 1)

            take_variance(dve, g, s.var)
            normalise(dve, g, 0, xn[:, :, :], s.rstd).then_inc(s.xn_ready, 1)
            for before, event in enumerate(Z_HEAD):
                if event == "max0":
                    for h in range(2 * GH):
                        for half in range(2):
                            row_max(0, h, half)
                z_event(event, 0, before)
            over_all(dve, iteration)



E1, I1 = 8, 4 * D
NI = I1 // P
NT = NB * NC
BIG = 3.0e38
COMBINE = 0.1


def moe_ffn(nc, g, ins, sem, tag, out=None):
    s = record(**{n: sem(f"{tag}_{n}") for n in (
        "var", "rstd", "w_in", "xn_ready", "xT_done", "xT_ready", "xT_stored", "logit_done", "logit_ready", "sig", "step",
        "counted", "wT_done", "wT_ready", "bias_done", "bias_free", "listed", "up_done", "gelu_done", "down_done",
        "acc_done", "x_done", "x_out", "fin")})
    load_in = [sem(f"{tag}_load{i}") for i in range(2)]
    with ExitStack() as ctx:
        def sb(name, shape, dt=F32, to=ctx):
            return to.enter_context(nc.sbuf_tensor(f"{tag}_{name}", shape, dt))

        def ps(name, shape, to):
            return to.enter_context(nc.psum_tensor(f"{tag}_{name}", shape, F32))

        xT_all = sb("xT_all", [P, NB, L])
        acc = sb("acc", [P, NT, D])
        logit = sb("logit", [P, NT, E1])
        w9 = sb("w9", [P, NT, E1 + 1])
        w_listed = sb("w_listed", [P, NT, E1])
        listed = sb("listed", [1, E1], mybir.dt.int32)
        pairs = sb("pairs", [1, 1], mybir.dt.int32)
        up = [sb(f"up{i}", [P, I1]) for i in range(2)]
        up_b = [sb(f"up_b{i}", [P, NI]) for i in range(2)]
        down = [sb(f"down{i}", [P, NI, D]) for i in range(2)]

        with ExitStack() as c1:
            gate = sb("gate", [P, E1], to=c1)
            gate_b = sb("gate_b", [P, E1], to=c1)
            xn = [sb(f"xn{i}", [P, NC, D], to=c1) for i in range(2)]
            xT = [sb(f"xT{i}", [P, L], to=c1) for i in range(2)]
            pT = [ps(f"pT{i}", [P, NC, P], c1) for i in range(2)]
            pL = [ps(f"pL{i}", [P, 512], c1) for i in range(2)]
            block = c1.enter_context(nc.Block())

            @block.sync
            def _(sp):
                sp.dma_start(gate[:, :], ins["L1_ffn_gate_w"]).then_inc(s.w_in, 16)
                sp.dma_start(gate_b[:, :], ins["L1_ffn_bias"].rearrange("(a e) -> a e", a=1).broadcast_to([P, E1])
                             ).then_inc(s.w_in, 16)
                sp.dma_start(up[0][:, :], ins["L1_ffn_sw_up"]).then_inc(load_in[0], 16)
                sp.dma_start(down[0][:, :, :], ins["L1_ffn_sw_down"].rearrange("(k i) h -> i k h", i=P)
                             ).then_inc(load_in[0], 16)
                sp.dma_start(up_b[0][:, :], ins["L1_ffn_sb_up"].rearrange("(k i) -> i k", i=P),
                             allow_slow_non_contiguous=True).then_inc(load_in[0], 16)

            @block.gpsimd
            def _(pool):
                take_rstd(pool, g, s.var, s.rstd)

            @block.tensor
            def _(pe):
                pe.wait_ge(s.w_in, 32)

                def step(new, old, par):
                    if old is not None:
                        pe.wait_ge(s.xT_ready, old + 1)
                        for c in range(NC):
                            last = pe.matmul(pL[1 - par][:, c * E1:(c + 1) * E1], xT[1 - par][:, c * P:(c + 1) * P],
                                             gate[:, :], start=True, stop=True)
                        last.then_inc(s.logit_done, 1)
                    if new is not None:
                        pe.wait_ge(s.xn_ready, new + 1)
                        for c in range(NC):
                            last = pe.transpose(pT[par][:, c, :], xn[par][:, c, :], g.identf[:, :])
                        last.then_inc(s.xT_done, 1)

                over_sequences(pe, step)

            @block.scalar
            def _(act):
                def step(new, old, par):
                    if new is not None:
                        act.wait_ge(s.xT_done, new + 1)
                        act.copy(xT[par][:, :], pT[par][:, :, :].rearrange("p c t -> p (c t)")
                                 ).then_inc(s.xT_ready, 1)

                over_sequences(act, step)

            @block.vector
            def _(dve):
                take_variance(dve, g, s.var)
                dve.wait_ge(s.w_in, 32)

                def step(new, old, par):
                    if new is not None:
                        normalise(dve, g, new, xn[par][:, :, :], s.rstd).then_inc(s.xn_ready, 1)
                    if old is not None:
                        dve.wait_ge(s.xT_ready, old + 1)
                        dve.tensor_scalar(xT_all[:, old, :], pT[1 - par][:, :, :].rearrange("p c t -> p (c t)"), 1.0,
                                          None, ALU.mult).then_inc(s.xT_stored, 1)
                        dve.wait_ge(s.logit_done, old + 1)
                        dve.tensor_tensor(logit[:, :, :].rearrange("p (b c) e -> p b c e", b=NB)[:, old, :, :],
                                          pL[1 - par][:, 0:NC * E1].rearrange("p (c e) -> p c e", c=NC),
                                          gate_b[:, :].unsqueeze(1).broadcast_to([P, NC, E1]), ALU.add
                                          ).then_inc(s.logit_ready, 1)

                over_sequences(dve, step)

        with ExitStack() as c2:
            ramp = sb("ramp", [P, E1], to=c2)
            index = sb("index", [1, E1], to=c2)
            sig = sb("sig", [P, NT, E1], to=c2)
            z2 = sb("z2", [P, NT, E1], to=c2)
            eq = sb("eq", [P, NT, E1], to=c2)
            hot = [sb(f"hot{i}", [P, NT, E1], to=c2) for i in range(2)]
            top = sb("top", [P, NT], to=c2)
            den = sb("den", [P, NT], to=c2)
            count = sb("count", [P, E1], to=c2)
            key = sb("key", [P, E1], to=c2)
            less = sb("less", [P, E1, E1], to=c2)
            rank = sb("rank", [P, E1], to=c2)
            place = sb("place", [P, E1, E1], to=c2)
            order = sb("order", [P, NT, E1, E1], to=c2)
            entry = sb("entry", [1, E1, E1], to=c2)
            listf = sb("listf", [1, E1], to=c2)
            pairsf = sb("pairsf", [1, 1], to=c2)
            more = sb("more", [1, 3], to=c2)
            limits = sb("limits", [1, 3], to=c2)
            biases = sb("biases", [E1 + 1, D], to=c2)
            wT = [sb(f"wT{i}", [E1 + 1, L], to=c2) for i in range(2)]
            pC = ps("pC", [P, 512], c2)
            pW = [ps(f"pW{i}", [P, NC, P], c2) for i in range(2)]
            pB = [ps(f"pB{i}", [P, NC, D], c2) for i in range(2)]
            block = c2.enter_context(nc.Block())

            @block.sync
            def _(sp):
                sp.dma_start(biases[0:E1, :], ins["L1_ffn_down_b"]).then_inc(s.w_in, 16)
                sp.dma_start(biases[E1:E1 + 1, :], ins["L1_ffn_sb_down"].rearrange("(a h) -> a h", a=1)
                             ).then_inc(s.w_in, 16)

            @block.gpsimd
            def _(pool):
                pool.iota(ramp[:, :], pattern=[[-1, E1]], base=E1, channel_multiplier=0,
                          allow_small_or_imprecise_dtypes=True)
                pool.memset(w9[:, :, E1:E1 + 1], 1.0).then_inc(s.fin, 1)
                pool.wait_ge(s.fin, 1)
                pool.iota(index[:, :], pattern=[[1, E1]], base=0, channel_multiplier=0,
                          allow_small_or_imprecise_dtypes=True).then_inc(s.fin, 1)
                pool.wait_ge(s.fin, 2)
                pool.iota(limits[:, :], pattern=[[2, 3]], base=2, channel_multiplier=0,
                          allow_small_or_imprecise_dtypes=True).then_inc(s.fin, 1)

            @block.scalar
            def _(act):
                act.activation(sig[:, :, :], logit[:, :, :], ACT.Sigmoid).then_inc(s.sig, 1)
                for b in range(NB):
                    act.wait_ge(s.wT_done, b + 1)
                    act.copy(wT[b % 2][:, :], pW[b % 2][0:E1 + 1, :, :].rearrange("e c t -> e (c t)")
                             ).then_inc(s.wT_ready, 1)

            @block.vector
            def _(dve):
                chain = Chain(dve, s.step, 31)
                chain.begin(0)
                link = chain.link

                def wide(tile):
                    return tile[:, :].unsqueeze(2).broadcast_to([P, NT, E1])

                def per_expert(row):
                    return row[:, :].unsqueeze(1).broadcast_to([P, NT, E1])

                dve.wait_ge(s.fin, 3)
                for i, z in enumerate((logit, z2)):
                    link(dve.tensor_reduce(top[:, :], z[:, :, :], AX.X, ALU.max))
                    link(dve.tensor_tensor(eq[:, :, :], z[:, :, :], wide(top), ALU.is_equal))
                    link(dve.tensor_tensor(eq[:, :, :], eq[:, :, :], per_expert(ramp), ALU.mult))
                    link(dve.tensor_reduce(top[:, :], eq[:, :, :], AX.X, ALU.max))
                    link(dve.tensor_tensor(hot[i][:, :, :], per_expert(ramp), wide(top), ALU.is_equal))
                    if i == 0:
                        link(dve.scalar_tensor_tensor(out=z2[:, :, :], in0=hot[0][:, :, :], scalar=-BIG,
                                                      in1=logit[:, :, :], op0=ALU.mult, op1=ALU.add))
                link(dve.tensor_tensor(hot[0][:, :, :], hot[0][:, :, :], hot[1][:, :, :], ALU.add))
                dve.wait_ge(s.sig, 1)
                link(dve.tensor_tensor(sig[:, :, :], sig[:, :, :], hot[0][:, :, :], ALU.mult))
                link(dve.tensor_reduce(den[:, :], sig[:, :, :], AX.X, ALU.add))
                link(dve.tensor_scalar(den[:, :], den[:, :], 1e-6, None, ALU.add))
                link(dve.reciprocal(den[:, :], den[:, :]))
                link(dve.tensor_tensor(w9[:, :, 0:E1], sig[:, :, :], wide(den), ALU.mult))
                link(dve.tensor_reduce(count[:, :], hot[0][:, :, :].rearrange("p t e -> p e t"), AX.X, ALU.add))
                dve.wait_ge(s.counted, 1)
                link(dve.tensor_scalar(key[:, :], pC[:, 0:E1], 0.0, -float(E1), ALU.is_gt, ALU.mult))
                link(dve.tensor_reduce(pairsf[:, :], key[0:1, :], AX.X, ALU.add))
                link(dve.tensor_scalar(pairsf[:, :], pairsf[:, :], -1.0 / E1, None, ALU.mult))
                link(dve.tensor_tensor(more[:, :], limits[:, :], pairsf[:, :].broadcast_to([1, 3]), ALU.is_lt))
                link(dve.tensor_reduce(pairsf[:, :], more[:, :], AX.X, ALU.add))
                link(dve.tensor_scalar(pairs[:, :], pairsf[:, :], 1.0, None, ALU.add))
                link(dve.tensor_tensor(key[:, :], key[:, :], ramp[:, :], ALU.subtract))
                link(dve.tensor_tensor(less[:, :, :], key[:, :].unsqueeze(1).broadcast_to([P, E1, E1]),
                                       key[:, :].unsqueeze(2).broadcast_to([P, E1, E1]), ALU.is_lt))
                link(dve.tensor_reduce(rank[:, :], less[:, :, :], AX.X, ALU.add))
                link(dve.tensor_scalar(rank[:, :], rank[:, :], -1.0, float(E1), ALU.mult, ALU.add))
                link(dve.tensor_tensor(place[:, :, :], ramp[:, :].unsqueeze(2).broadcast_to([P, E1, E1]),
                                       rank[:, :].unsqueeze(1).broadcast_to([P, E1, E1]), ALU.is_equal))
                link(dve.tensor_tensor(entry[:, :, :], place[0:1, :, :],
                                       index[:, :].unsqueeze(1).broadcast_to([1, E1, E1]), ALU.mult))
                link(dve.tensor_reduce(listf[:, :], entry[:, :, :], AX.X, ALU.add))
                chain.end()
                dve.tensor_copy(listed[:, :], listf[:, :])
                for r in range(E1):
                    last = dve.tensor_tensor(order[:, :, r, :], w9[:, :, 0:E1],
                                             place[:, r, :].unsqueeze(1).broadcast_to([P, NT, E1]), ALU.mult)
                last.then_inc(s.listed, 1)
                dve.wait_ge(s.listed, 1)
                dve.tensor_reduce(w_listed[:, :, :], order[:, :, :, :], AX.X, ALU.add)
                for b in range(NB):
                    dve.wait_ge(s.bias_done, b + 1)
                    dve.tensor_copy(acc[:, b * NC:(b + 1) * NC, :], pB[b % 2][:, :, :]).then_inc(s.bias_free, 1)

            @block.tensor
            def _(pe):
                pe.wait_ge(s.step, 18)
                pe.matmul(pC[:, 0:E1], g.onesf[:, :], count[:, :], start=True, stop=True).then_inc(s.counted, 1)
                pe.wait_ge(s.w_in, 64)
                for b in range(NB):
                    if b >= 2:
                        pe.wait_ge(s.wT_ready, b - 1)
                    for c in range(NC):
                        last = pe.transpose(pW[b % 2][0:E1 + 1, c, :], w9[:, b * NC + c, :], g.identf[:, :])
                    last.then_inc(s.wT_done, 1)
                    pe.wait_ge(s.wT_ready, b + 1)
                    if b >= 2:
                        pe.wait_ge(s.bias_free, b - 1)
                    for c in range(NC):
                        last = pe.matmul(pB[b % 2][:, c, :], wT[b % 2][:, c * P:(c + 1) * P], biases[:, :],
                                         start=True, stop=True)
                    last.then_inc(s.bias_done, 1)

        with ExitStack() as c3:
            hidden = [sb(f"hidden{i}", [P, NI, L], to=c3) for i in range(2)]
            pU = [ps(f"pU{i}", [P, L], c3) for i in range(NI)]
            pD = [ps(f"pD{i}", [P, NC, D], c3) for i in range(2)]
            block = c3.enter_context(nc.Block())

            def over_experts(eng, expert):
                expert(0, 0, None, None)
                trips = eng.value_load(pairs[0:1, 0:1], min_val=1, max_val=E1 // 2)
                with eng.Fori(0, trips) as i:
                    expert(2 * i + 1, 1, 2 * i, i)
                    expert(2 * i + 2, 0, 2 * i + 1, i)

            @block.sync
            def _(sp):
                def expert(n, buf, place, trip):
                    if place is None:
                        return
                    e = sp.value_load(listed[0:1, bass.ds(place, 1)], min_val=0, max_val=E1 - 1)
                    if buf == 0:
                        sp.wait_ge(s.down_done, NB * n - NB)
                    else:
                        sp.wait_ge(s.down_done, NB * n)
                    sp.dma_start(up[buf][:, :], ins["L1_ffn_up_w"][e]).then_inc(load_in[buf], 16)
                    sp.dma_start(down[buf][:, :, :], ins["L1_ffn_down_w"][e].rearrange("(k i) h -> i k h", i=P)
                                 ).then_inc(load_in[buf], 16)
                    sp.dma_start(up_b[buf][:, :], ins["L1_ffn_up_b"][e].rearrange("(k i) -> i k", i=P),
                                 allow_slow_non_contiguous=True).then_inc(load_in[buf], 16)

                over_experts(sp, expert)

            @block.tensor
            def _(pe):
                def up_product(n, buf, t):
                    m = NB * n + t
                    for k in range(NI):
                        if not isinstance(m, int) or m > 0:
                            pe.wait_ge(s.gelu_done, NI * m + k + 1 - NI)
                        pe.matmul(pU[k][:, :], up[buf][:, k * P:(k + 1) * P], xT_all[:, t, :],
                                  start=True, stop=True).then_inc(s.up_done, 1)

                def down_product(n, buf, t):
                    m = NB * n + t
                    pe.wait_ge(s.gelu_done, NI * m + NI)
                    if not isinstance(m, int) or m > 1:
                        pe.wait_ge(s.acc_done, m - 1)
                    for c in range(NC):
                        for k in range(NI):
                            last = pe.matmul(pD[t % 2][:, c, :], hidden[t % 2][:, k, c * P:(c + 1) * P],
                                             down[buf][:, k, :], start=(k == 0), stop=(k == NI - 1))
                    last.then_inc(s.down_done, 1)

                def expert(n, buf, place, trip):
                    loads = 1 if trip is None else trip + 2 - buf
                    pe.wait_ge(load_in[buf], 48 * loads)
                    for t in range(NB + 1):
                        if t < NB:
                            up_product(n, buf, t)
                        if t > 0:
                            down_product(n, buf, t - 1)

                over_experts(pe, expert)

            @block.scalar
            def _(act):
                def expert(n, buf, place, trip):
                    for t in range(NB):
                        for k in range(NI):
                            act.wait_ge(s.up_done, NI * (NB * n + t) + k + 1)
                            act.activation(hidden[t % 2][:, k, :], pU[k][:, :], ACT.Gelu, bias=up_b[buf][:, k:k + 1]
                                           ).then_inc(s.gelu_done, 1)

                over_experts(act, expert)

            @block.vector
            def _(dve):
                def expert(n, buf, place, trip):
                    for t in range(NB):
                        m = NB * n + t
                        dve.wait_ge(s.down_done, m + 1)
                        tiles = slice(t * NC, (t + 1) * NC)
                        if place is None:
                            last = dve.tensor_tensor(acc[:, tiles, :], pD[t % 2][:, :, :], acc[:, tiles, :], ALU.add)
                        else:
                            for c in range(NC):
                                at = acc[:, t * NC + c, :]
                                last = dve.scalar_tensor_tensor(
                                    out=at, in0=pD[t % 2][:, c, :],
                                    scalar=w_listed[:, t * NC + c, bass.ds(place, 1)], in1=at,
                                    op0=ALU.mult, op1=ALU.add)
                        last.then_inc(s.acc_done, 1)

                over_experts(dve, expert)

        with ExitStack() as c4:
            top = sb("max", [P, NT], to=c4)
            block = c4.enter_context(nc.Block())

            @block.vector
            def _(dve):
                chain = Chain(dve, s.fin, 3)
                chain.begin(1)
                link = chain.link
                link(dve.tensor_reduce(top[:, :], acc[:, :, :], AX.X, ALU.max, apply_absolute_value=True))
                link(dve.tensor_scalar(top[:, :], top[:, :], COMBINE, 1e-6, ALU.mult, ALU.add))
                link(dve.reciprocal(top[:, :], top[:, :]))
                link_scale = dve.tensor_scalar(top[:, :], top[:, :], 0.5 * COMBINE, None, ALU.mult)
                link_scale.then_inc(s.x_done, 1)
                dve.wait_ge(s.x_done, 1)
                for b in range(NB):
                    for c in range(NC):
                        x = g.X[:, b, c, :]
                        last = dve.scalar_tensor_tensor(out=x, in0=acc[:, b * NC + c, :],
                                                        scalar=top[:, b * NC + c:b * NC + c + 1], in1=x,
                                                        op0=ALU.mult, op1=ALU.add)
                    last.then_inc(s.x_done, 1)
                    if out is None:
                        take_stats(dve, g, b, s.x_done, b + 2)

            if out is not None:
                @block.sync
                def _(sp):
                    for b in range(NB):
                        sp.wait_ge(s.x_done, b + 2)
                        sp.dma_start(out[b].rearrange("(c p) d -> p c d", p=P), g.X[:, b]).then_inc(s.x_out, 16)
                    sp.wait_ge(s.x_out, 16 * NB)



NS = 16
RT = 64
RING = 4
LEAD = 3
QROWS = 32


def selective_scan(nc, g, ins, sem, tag):
    s = record(**{n: sem(f"{tag}_{n}") for n in (
        "var", "rstd", "w_in", "made", "a_exp", "xn_ready", "xT_done", "xT_ready", "u_done", "e_ready", "e1_ready", "inv", "us_ready",
        "bc_done", "bc_ready", "dt1_ready", "lin_done", "w_ready", "ln_ready", "e_dt", "nd_ready", "r_ready",
        "rest_ready", "mid_ready", "split_ready", "corr_ready", "dt_ready", "xdt_ready", "b_bcast", "c_bcast", "c_ready", "alpha_ready",
        "beta", "h_ready", "hc_ready", "hc_used", "y_free", "selected", "a_made")})
    with ExitStack() as ctx:
        def sb(name, shape, dt=F32):
            return ctx.enter_context(nc.sbuf_tensor(f"{tag}_{name}", shape, dt))

        def ps(name, shape):
            return ctx.enter_context(nc.psum_tensor(f"{tag}_{name}", shape, F32))

        kT, dcoef, a_log, a_neg = sb("kT", [P, 3]), sb("dcoef", [P, 1]), sb("a_log", [P, NS]), sb("a_neg", [P, NS])
        w_bc, b_bc = sb("w_bc", [P, 3, QROWS]), sb("b_bc", [3 * QROWS, 1])
        w_dt, b_dt, w_dtp, b_dtp = sb("w_dt", [P, RT]), sb("b_dt", [RT, 1]), sb("w_dtp", [RT, D]), sb("b_dtp", [P, 1])
        diag_k, diag_d = sb("diag_k", [P, 3, P]), sb("diag_d", [P, P])
        pick = sb("pick", [3 * QROWS, QROWS])
        select = sb("select", [3 * QROWS, QROWS, P], BF16)
        zeros = sb("zeros", [1, P + L], BF16)

        xn = [sb(f"xn{i}", [P, NC, D]) for i in range(2)]
        xT = [sb(f"xT{i}", [P, L + 2]) for i in range(2)]
        parts = [sb(f"parts{i}", [3 * QROWS, L], BF16) for i in range(2)]
        dt = [sb(f"dt_of{i}", [P, L]) for i in range(2)]
        xdt = [sb(f"xdt{i}", [P, L]) for i in range(2)]
        e, e1, inv, us = (sb(n, [P, L]) for n in ("e", "e1", "inv", "us"))
        bc, bc_rest, dt1 = sb("bc", [3 * QROWS, L]), sb("bc_rest", [2 * QROWS, L]), sb("dt_low", [RT, L])
        edt, w1, lnw, nd, rw, corr = (sb(n, [P, L]) for n in ("edt", "w1", "lnw", "nd", "rw", "corr"))
        alpha, beta, h, c_sb, hc = ([sb(f"{n}{i}", [P, L]) for i in range(RING)] for n in ("alpha", "beta", "h", "c", "hc"))

        pF = [ps(f"pF{i}", [P, L]) for i in range(2)]
        pB = [ps(f"pB{i}", [P, L]) for i in range(2)]
        pC = [ps(f"pC{i}", [P, L]) for i in range(2)]
        pY = [ps(f"pY{i}", [P, NC, D]) for i in range(2)]

        def column(a):
            return a.rearrange("(p a) -> p a", a=1)

        def over_steps(eng, step):
            step(0, None, None, 0)
            step(1, 0, None, 1)
            with eng.Fori(0, NB // 2 - 1) as i:
                step(2 * i + 2, 2 * i + 1, 2 * i, 0)
                step(2 * i + 3, 2 * i + 2, 2 * i + 1, 1)
            step(None, NB - 1, NB - 2, 0)
            step(None, None, NB - 1, 1)

        def wait_for(eng, sem_, b, n):
            if not (isinstance(b, int) and b * NS + n < 0):
                eng.wait_ge(sem_, b * NS + n + 1)

        block = ctx.enter_context(nc.Block())

        @block.sync
        def _(sp):
            sp.dma_start(kT[:, :], ins["L1_attn_conv_kernel"].rearrange("k a d -> d (k a)"),
                         allow_slow_non_contiguous=True).then_inc(s.w_in, 16)
            sp.dma_start(dcoef[:, :], column(ins["L1_attn_Dcoeff"]), allow_slow_non_contiguous=True).then_inc(s.w_in, 16)
            sp.dma_start(a_log[:, :], ins["L1_attn_A_log"]).then_inc(s.w_in, 16)
            for k in range(3):
                sp.dma_start(w_bc[:, k, :], ins["L1_attn_W_bc"]).then_inc(s.w_in, 16)
                sp.dma_start(b_bc[k * QROWS:(k + 1) * QROWS, :], column(ins["L1_attn_b_bc"]),
                             allow_slow_non_contiguous=True).then_inc(s.w_in, 16)
            sp.dma_start(w_dt[:, :], ins["L1_attn_W_dt"]).then_inc(s.w_in, 16)
            sp.dma_start(w_dtp[:, :], ins["L1_attn_W_dtp"]).then_inc(s.w_in, 16)
            sp.dma_start(b_dt[:, :], column(ins["L1_attn_b_dt"]), allow_slow_non_contiguous=True).then_inc(s.w_in, 16)
            sp.dma_start(b_dtp[:, :], column(ins["L1_attn_b_dtp"]), allow_slow_non_contiguous=True
                         ).then_inc(s.w_in, 16)

        ALL_IN = 13 * 16

        @block.gpsimd
        def _(pool):
            take_rstd(pool, g, s.var, s.rstd)
            pool.memset(xT[0][:, :], 0.0)
            pool.memset(xT[1][:, :], 0.0)
            pool.memset(zeros[:, :], 0.0)
            pool.memset(pick[:, :], 0.0).then_inc(s.made, 1)
            for k in range(3):
                pool.wait_ge(s.made, k + 1)
                pool.affine_select(out=pick[:, :], in_=pick[:, :], compare_op=ALU.not_equal, fill=1.0,
                                   base=-k * QROWS, pattern=[[-1, QROWS]], channel_multiplier=1).then_inc(s.made, 1)
            pool.wait_ge(s.w_in, ALL_IN)
            for k in range(3):
                pool.tensor_scalar(diag_k[:, k, :], g.identf[:, :], kT[:, k:k + 1], None, ALU.mult)
            pool.tensor_scalar(diag_d[:, :], g.identf[:, :], dcoef[:, :], None, ALU.mult).then_inc(s.made, 1)
            pool.wait_ge(s.a_exp, 1)
            pool.tensor_scalar(a_neg[:, :], a_log[:, :], -1.0, None, ALU.mult).then_inc(s.a_made, 1)

            def inputs(b, par, n):
                if n == 9:
                    pool.wait_ge(s.bc_ready, b + 1)
                    pool.tensor_tensor(bc_rest[:, :], bc[0:2 * QROWS, :], parts[par][0:2 * QROWS, :], ALU.subtract
                                       ).then_inc(s.rest_ready, 1)
                if n == 11:
                    pool.wait_ge(s.mid_ready, b + 1)
                    pool.tensor_tensor(parts[par][0:QROWS, :], bc_rest[0:QROWS, :], parts[par][0:QROWS, :],
                                       ALU.subtract).then_inc(s.split_ready, 1)
                if n == 13:
                    pool.wait_ge(s.corr_ready, b + 1)
                    pool.tensor_tensor(dt[par][:, :], lnw[:, :], corr[:, :], ALU.subtract).then_inc(s.dt_ready, 1)

            def step(new, old, older, par):
                for n in range(NS):
                    if new is not None:
                        inputs(new, par, n)
                    if old is not None:
                        wait_for(pool, s.h_ready, old, n)
                        wait_for(pool, s.c_ready, old, n)
                        wait_for(pool, s.hc_used, old, n - RING)
                        pool.tensor_tensor(hc[n % RING][:, :], h[n % RING][:, :], c_sb[n % RING][:, :], ALU.mult
                                           ).then_inc(s.hc_ready, 1)

            over_steps(pool, step)

        @block.tensor
        def _(pe):
            pe.wait_ge(s.w_in, ALL_IN)
            pe.wait_ge(s.made, 5)
            pe.wait_ge(s.selected, 1)

            def inputs(b, par, n):
                if n == 1:
                    pe.wait_ge(s.xn_ready, b + 1)
                    for c in range(NC):
                        last = pe.transpose(pF[0][:, c * P:(c + 1) * P], xn[par][:, c, :], g.identf[:, :])
                    last.then_inc(s.xT_done, 1)
                if n == 3:
                    pe.wait_ge(s.xT_ready, b + 1)
                    for k in range(3):
                        last = pe.matmul(pF[1][:, :], diag_k[:, k, :], xT[par][:, k:k + L], start=(k == 0), stop=(k == 2))
                    last.then_inc(s.u_done, 1)
                if n == 6:
                    pe.wait_ge(s.us_ready, b + 1)
                    pe.matmul(pF[0][0:3 * QROWS, :], w_bc[:, :, :].rearrange("d k r -> d (k r)"), us[:, :],
                              start=True, stop=True)
                    pe.matmul(pF[1][0:RT, :], w_dt[:, :], us[:, :], start=True, stop=True).then_inc(s.bc_done, 1)
                if n == 8:
                    pe.wait_ge(s.dt1_ready, b + 1)
                    pe.wait_ge(s.bc_ready, b + 1)
                    pe.matmul(pF[0][:, :], w_dtp[:, :], dt1[:, :], start=True, stop=True).then_inc(s.lin_done, 1)

            def broadcast(b, par, n):
                if n == 0:
                    pe.wait_ge(s.split_ready, b + 1)
                wait_for(pe, s.beta, b, n - 2)
                pe.matmul(pB[n % 2][:, :], select[:, n, :], parts[par][:, :], start=True, stop=True
                          ).then_inc(s.b_bcast, 1)
                wait_for(pe, s.c_ready, b, n - 2)
                pe.matmul(pC[n % 2][:, :], select[:, NS + n, :], parts[par][:, :], start=True, stop=True
                          ).then_inc(s.c_bcast, 1)

            def add_state(b, par, n):
                if n == 0:
                    pe.wait_ge(s.y_free, b + 1)
                    pe.matmul(pY[par][:, :, :], zeros[:, 0:P], zeros[:, P:P + L], start=True, stop=False)
                    for c in range(NC):
                        pe.matmul(pY[par][:, c, :], xT[par][:, 1 + c * P:1 + (c + 1) * P], diag_d[:, :],
                                  start=False, stop=False)
                wait_for(pe, s.hc_ready, b, n)
                for c in range(NC):
                    last = pe.matmul(pY[par][:, c, :], hc[n % RING][:, c * P:(c + 1) * P], g.identf[:, :],
                                     start=False, stop=(n == NS - 1 and c == NC - 1))
                last.then_inc(s.hc_used, 1)

            def step(new, old, older, par):
                for n in range(NS):
                    if new is not None:
                        inputs(new, par, n)
                    if old is not None:
                        broadcast(old, 1 - par, n)
                    if n < LEAD and older is not None:
                        add_state(older, par, NS - LEAD + n)
                    if n >= LEAD and old is not None:
                        add_state(old, 1 - par, n - LEAD)

            over_steps(pe, step)

        @block.scalar
        def _(act):
            act.preload_act_table_set("natural_log_exp_and_others")
            act.wait_ge(s.w_in, ALL_IN)
            act.activation(a_log[:, :], a_log[:, :], ACT.Exp).then_inc(s.a_exp, 1)
            act.wait_ge(s.a_made, 1)

            def inputs(b, par, n):
                if n == 2:
                    act.wait_ge(s.xT_done, b + 1)
                    act.copy(xT[par][:, 1:L + 1], pF[0][:, :]).then_inc(s.xT_ready, 1)
                if n == 4:
                    act.wait_ge(s.u_done, b + 1)
                    act.activation(e[:, :], pF[1][:, :], ACT.Exp, scale=-1.0).then_inc(s.e_ready, 1)
                    act.wait_ge(s.e_ready, b + 1)
                    act.activation(e1[:, :], e[:, :], ACT.Ln, bias=1.0).then_inc(s.e1_ready, 1)
                    act.wait_ge(s.e1_ready, b + 1)
                    act.activation(inv[:, :], e1[:, :], ACT.Exp, scale=-1.0).then_inc(s.inv, 1)
                if n == 7:
                    act.wait_ge(s.bc_done, b + 1)
                    act.activation(dt1[:, :], pF[1][0:RT, :], ACT.Identity, bias=b_dt[:, :]).then_inc(s.dt1_ready, 1)
                    act.activation(parts[par][:, :], pF[0][0:3 * QROWS, :], ACT.Identity, bias=b_bc[:, :])
                    act.activation(bc[:, :], pF[0][0:3 * QROWS, :], ACT.Identity, bias=b_bc[:, :]
                                   ).then_inc(s.bc_ready, 1)
                if n == 9:
                    act.wait_ge(s.lin_done, b + 1)
                    act.activation(edt[:, :], pF[0][:, :], ACT.Exp, bias=b_dtp[:, :]).then_inc(s.e_dt, 1)
                    act.wait_ge(s.e_dt, b + 1)
                    act.activation(w1[:, :], edt[:, :], ACT.Identity, bias=1.0).then_inc(s.w_ready, 1)
                if n == 10:
                    act.wait_ge(s.w_ready, b + 1)
                    act.activation(lnw[:, :], w1[:, :], ACT.Ln).then_inc(s.ln_ready, 1)
                    act.wait_ge(s.rest_ready, b + 1)
                    act.copy(parts[par][0:2 * QROWS, :], bc_rest[:, :]).then_inc(s.mid_ready, 1)
                if n == 11:
                    act.wait_ge(s.ln_ready, b + 1)
                    act.activation(rw[:, :], lnw[:, :], ACT.Exp, scale=-1.0).then_inc(s.r_ready, 1)

            def step(new, old, older, par):
                for n in range(NS):
                    if new is not None:
                        inputs(new, par, n)
                    if old is not None:
                        if n == 0:
                            act.wait_ge(s.dt_ready, old + 1)
                        wait_for(act, s.h_ready, old, n - RING)
                        act.activation(alpha[n % RING][:, :], dt[1 - par][:, :], ACT.Exp, scale=a_neg[:, n:n + 1]
                                       ).then_inc(s.alpha_ready, 1)
                        wait_for(act, s.c_bcast, old, n)
                        wait_for(act, s.hc_ready, old, n - RING)
                        act.copy(c_sb[n % RING][:, :], pC[n % 2][:, :]).then_inc(s.c_ready, 1)

            over_steps(act, step)

        @block.vector
        def _(dve):
            dve.sem_inc(s.y_free, 2)
            take_variance(dve, g, s.var)
            dve.wait_ge(s.made, 4)
            dve.tensor_copy(select[:, :, :], pick[:, :].unsqueeze(2).broadcast_to([3 * QROWS, QROWS, P])
                            ).then_inc(s.selected, 1)

            def inputs(b, par, n):
                if n == 0:
                    normalise(dve, g, b, xn[par], s.rstd).then_inc(s.xn_ready, 1)
                if n == 5:
                    dve.wait_ge(s.inv, b + 1)
                    dve.tensor_tensor(us[:, :], pF[1][:, :], inv[:, :], ALU.mult).then_inc(s.us_ready, 1)
                if n == 11:
                    dve.wait_ge(s.w_ready, b + 1)
                    dve.scalar_tensor_tensor(out=nd[:, :], in0=w1[:, :], scalar=-1.0, in1=edt[:, :],
                                             op0=ALU.add, op1=ALU.subtract).then_inc(s.nd_ready, 1)
                if n == 12:
                    dve.wait_ge(s.nd_ready, b + 1)
                    dve.wait_ge(s.r_ready, b + 1)
                    dve.tensor_tensor(corr[:, :], nd[:, :], rw[:, :], ALU.mult).then_inc(s.corr_ready, 1)
                if n == 14:
                    dve.wait_ge(s.dt_ready, b + 1)
                    dve.tensor_tensor(xdt[par][:, :], xT[par][:, 1:L + 1], dt[par][:, :], ALU.mult
                                      ).then_inc(s.xdt_ready, 1)

            def scan(b, n):
                wait_for(dve, s.beta, b, n)
                wait_for(dve, s.alpha_ready, b, n)
                wait_for(dve, s.hc_ready, b, n - RING)
                dve.tensor_tensor_scan(h[n % RING][:, :], alpha[n % RING][:, :], beta[n % RING][:, :], 0.0,
                                       ALU.mult, ALU.add).then_inc(s.h_ready, 1)

            def step(new, old, older, par):
                for n in range(NS):
                    if new is not None:
                        inputs(new, par, n)
                    if n == LEAD + 1 and older is not None:
                        wait_for(dve, s.hc_used, older, NS - 1)
                        dve.tensor_tensor(g.X[:, older, :, :], g.X[:, older, :, :], pY[par][:, :, :], ALU.add
                                          ).then_inc(s.y_free, 1)
                        take_stats(dve, g, older, s.y_free, older + 3)
                    if old is not None:
                        if n == 0:
                            dve.wait_ge(s.xdt_ready, old + 1)
                        wait_for(dve, s.b_bcast, old, n)
                        wait_for(dve, s.h_ready, old, n - RING)
                        dve.tensor_tensor(beta[n % RING][:, :], pB[n % 2][:, :], xdt[1 - par][:, :], ALU.mult
                                          ).then_inc(s.beta, 1)
                        if n:
                            scan(old, n - 1)
                if old is not None:
                    scan(old, NS - 1)

            over_steps(dve, step)


def macaron(nc, ins, out):
    with ExitStack() as ctx:
        def sb(name, shape, dt=F32):
            return ctx.enter_context(nc.sbuf_tensor(name, shape, dt))

        taken = []

        def sem(name):
            taken.append(nc.alloc_semaphore(name=name))
            return taken[-1]

        g = record(
            X=sb("X", [P, NB, NC, D]), mean=sb("mean", [P, NB, NC]), rstd=sb("rstd", [P, NB, NC]),
            ln_t=sb("ln_t", [P, NB, NC]), ln_u=sb("ln_u", [P, NB, NC]), bn6=sb("bn6", [P, NB, NC, 6]),
            carrier=sb("carrier", [P, NB, 1]), identf=sb("identf", [P, P]),
            onesf=sb("onesf", [P, P]), neghalf=sb("neghalf", [P, NB, NC]))
        w = record(
            wd1=sb("wd1", [P, E0, H0]), bd1=sb("bd1", [1, E0 * H0]), wbase=sb("wbase", [P, D]),
            sel=sb("adapters", [P, E0, WSEL]), b2T=sb("b2T", [P, E0]), b2_slope=sb("b2_slope", [P, E0]),
            b2_const=sb("b2_const", [P, E0]), loss=sb("loss_weights", [P, 2, LOSSCOL]),
            expert_mask=sb("expert_mask", [P, 2, E0]), down_count=sb("down_count", [P, E0]),
            wT=sb("wT", [P, 4, D]), bo=sb("bo", [1, D]))
        set_up(nc, g, ins, sem)
        adapter_weights(nc, g, w, ins, sem)
        attention_weights(nc, g, w, ins, sem)
        adapter_ffn(nc, g, w, sem, "f1")
        attention(nc, g, w, sem)
        nc.all_engine_barrier()
        nc.clear_and_free_semaphores(taken)
        nc.all_engine_barrier()
        adapter_ffn(nc, g, w, sem, "f2")
        moe_ffn(nc, g, ins, sem, "m1")
        selective_scan(nc, g, ins, sem, "ss")
        moe_ffn(nc, g, ins, sem, "m2", out=out)


_INS = ['L0_attn_x', 'L0_attn_qkv_weight', 'L0_attn_qkv_weight_mask', 'L0_attn_out_weight', 'L0_attn_out_weight_mask',
        'L0_attn_out_bias', 'L0_attn_out_bias_mask', 'L0_ffn_W_base', 'L0_ffn_b_base', 'L0_ffn_Wd1', 'L0_ffn_bd1',
        'L0_ffn_Wd2', 'L0_ffn_bd2', 'L0_ffn_Wa_down', 'L0_ffn_ba_down', 'L0_ffn_Wa_up', 'L0_ffn_ba_up',
        'L1_attn_conv_kernel', 'L1_attn_A_log', 'L1_attn_W_bc', 'L1_attn_b_bc', 'L1_attn_Dcoeff', 'L1_attn_W_dt',
        'L1_attn_b_dt', 'L1_attn_W_dtp', 'L1_attn_b_dtp', 'L1_ffn_gate_w', 'L1_ffn_bias', 'L1_ffn_up_w', 'L1_ffn_up_b',
        'L1_ffn_down_w', 'L1_ffn_down_b', 'L1_ffn_sw_up', 'L1_ffn_sb_up', 'L1_ffn_sw_down', 'L1_ffn_sb_down']
_OUTS = [((NB, L, D), 'float32')]


def kernel(**inputs):
    import numpy as _np
    import concourse.bacc as _bacc
    from concourse import mybir as _mybir
    from concourse.bass_utils import run_bass_kernel_spmd as _run

    nc = _bacc.Bacc("TRN2", target_bir_lowering=False, num_devices=1)
    arrays, ins = {}, {}
    for name in _INS:
        a = _np.ascontiguousarray(inputs[name])
        arrays[f"in_{name}_dram"] = a
        ins[name] = nc.dram_tensor(f"in_{name}_dram", a.shape, _mybir.dt.from_np(a.dtype), kind="ExternalInput").ap()
    shape, dtype = _OUTS[0]
    out = nc.dram_tensor("out_0_dram", shape, _mybir.dt.from_np(_np.dtype(dtype)), kind="ExternalOutput").ap()
    macaron(nc, ins, out)
    r = _run(nc, [arrays], core_ids=[0])
    return r.results[0]["out_0_dram"]
```

```python
from collections import namedtuple
from contextlib import ExitStack

import concourse.bass as bass
from concourse import mybir

ALU = mybir.AluOpType
ACT = mybir.ActivationFunctionType
AX = mybir.AxisListType
F32 = mybir.dt.float32
BF16 = mybir.dt.bfloat16

P = 128
NB, L, D = 8, 512, 128
NC = L // P
EPS = 1e-5


def record(**named):
    return namedtuple("Record", named)(**named)


def over_sequences(eng, step):
    step(0, None, 0)
    with eng.Fori(0, NB // 2 - 1) as i:
        step(2 * i + 1, 2 * i, 1)
        step(2 * i + 2, 2 * i + 1, 0)
    step(NB - 1, NB - 2, 1)
    step(None, NB - 1, 0)


class Chain:

    def __init__(self, eng, sem, per):
        self.eng, self.sem, self.per = eng, sem, per

    def begin(self, b):
        self.at, self.n = b * self.per, 0

    def link(self, ins):
        self.n += 1
        ins.then_inc(self.sem, 1)
        self.eng.wait_ge(self.sem, self.at + self.n)

    def end(self):
        assert self.n == self.per, (self.n, self.per)



def set_up(block, g, ins, sem):
    x_in = [sem(f"x{b}_in") for b in range(NB)]
    made = g.consts_made

    @block.sync
    def _(sp):
        for b in range(NB):
            sp.dma_start(g.X[:, b], ins["L0_attn_x"][b].rearrange("(c p) d -> p c d", p=P)).then_inc(x_in[b], 16)

    @block.gpsimd
    def _(pool):
        pool.memset(g.identf[:, :], 0.0).then_inc(made, 1)
        pool.memset(g.onesf[:, :], 1.0)
        pool.memset(g.neghalf[:, :, :], -0.5).then_inc(made, 1)
        pool.wait_ge(made, 2)
        pool.affine_select(out=g.identf[:, :], in_=g.identf[:, :], compare_op=ALU.not_equal, fill=1.0,
                           base=0, pattern=[[-1, P]], channel_multiplier=1).then_inc(made, 1)

    @block.vector
    def _(dve):
        for b in range(NB):
            take_stats(dve, g, b, x_in[b], 16)


def take_stats(dve, g, b, x_done, n):
    dve.wait_ge(x_done, n)
    dve.tensor_scalar(g.carrier[:, b, :], g.X[:, b, 0, 0:1], 1.0, None, ALU.mult)
    for c in range(NC):
        last = dve.bn_stats(g.bn6[:, b, c, :], g.X[:, b, c, :])
    return last


def take_variance(dve, g, step):
    even, odd = (lambda k: g.bn6[:, :, :, k]), (lambda k: g.bn6[:, :, :, 3 + k])
    t, u = g.ln_t, g.ln_u
    dve.tensor_tensor(g.mean[:, :, :], even(1), odd(1), ALU.add)
    dve.tensor_tensor(t[:, :, :], even(1), odd(1), ALU.subtract)
    dve.tensor_tensor(u[:, :, :], even(2), odd(2), ALU.add).then_inc(step, 1)
    dve.wait_ge(step, 1)
    dve.scalar_tensor_tensor(out=t[:, :, :], in0=t[:, :, :], scalar=0.25, in1=t[:, :, :], op0=ALU.mult, op1=ALU.mult)
    dve.tensor_scalar(u[:, :, :], u[:, :, :], 1.0 / D, EPS, ALU.mult, ALU.add)
    dve.tensor_scalar(g.mean[:, :, :], g.mean[:, :, :], 0.5, None, ALU.mult).then_inc(step, 1)
    dve.wait_ge(step, 2)
    dve.tensor_tensor(u[:, :, :], u[:, :, :], t[:, :, :], ALU.add).then_inc(step, 1)


def take_rstd(pool, g, step, ready, others=None):
    pool.wait_ge(step, 3)
    pool.tensor_tensor(g.rstd[:, 0, :], g.ln_u[:, 0, :], g.neghalf[:, 0, :], ALU.pow).then_inc(ready, 1)
    if others is not None:
        others()
    pool.tensor_tensor(g.rstd[:, 1:NB, :], g.ln_u[:, 1:NB, :], g.neghalf[:, 1:NB, :], ALU.pow).then_inc(ready, NB - 1)


def normalise(dve, g, b, out, rstd_ready):
    dve.wait_ge(rstd_ready, b + 1)
    for c in range(NC):
        last = dve.tensor_scalar(out[:, c, :], g.X[:, b, c, :], g.mean[:, b, c:c + 1], g.rstd[:, b, c:c + 1],
                                 ALU.subtract, ALU.mult)
    return last



E0, H0, R0 = 8, 32, 64
HALF = E0 // 2
WSEL = R0 + D + 1
BIAS_ROWS = 96
LOSSCOL = P + D + 1


def adapter_weights(block, ctx, nc, g, w, ins, sem):
    ld = sem("aw_loaded")
    ld2 = sem("aw_bias_loaded")
    mk = sem("aw_masks")
    tr = sem("aw_transposed")
    cp = sem("aw_copied")
    mm = sem("aw_products")
    st = sem("aw_steps")
    bp = sem("aw_bias_parts")
    w2 = ctx.enter_context(nc.sbuf_tensor("aw_w2", [P, 2, D], F32))
    w2T = ctx.enter_context(nc.sbuf_tensor("aw_w2T", [P, 2, P], F32))
    block_mask = ctx.enter_context(nc.sbuf_tensor("aw_block", [P, HALF, H0], F32))
    base_row = ctx.enter_context(nc.sbuf_tensor("aw_base", [1, D], F32))
    base_at = ctx.enter_context(nc.sbuf_tensor("aw_base_at", [R0 + 1, D], F32))
    junk = ctx.enter_context(nc.sbuf_tensor("aw_junk", [P, E0], F32))
    bd1 = ctx.enter_context(nc.sbuf_tensor("aw_bd1", [BIAS_ROWS, E0 * H0], F32))
    bd1_rest = ctx.enter_context(nc.sbuf_tensor("aw_bd1_rest", [64, E0 * H0], F32))
    pT = ctx.enter_context(nc.psum_tensor("aw_pT", [P, 2, 512], F32))
    pW = ctx.enter_context(nc.psum_tensor("aw_pW", [P, 2, 512], F32))
    pB = ctx.enter_context(nc.psum_tensor("aw_pB", [P, 2, 512], F32))

    @block.sync
    def _(sp):
        sp.dma_start(w2[:, :, :], ins["L0_ffn_Wd2"].rearrange("(g e) h d -> (e h) g d", g=2)).then_inc(ld, 16)
        sp.dma_start(w.wd1[:, :, :], ins["L0_ffn_Wd1"].rearrange("e d h -> d e h")).then_inc(ld, 16)
        sp.dma_start(w.sel[:, :, 0:R0], ins["L0_ffn_Wa_down"].rearrange("e d r -> d e r")).then_inc(ld, 16)
        sp.dma_start(w.wbase[:, :], ins["L0_ffn_W_base"]).then_inc(ld, 16)

    @block.scalar
    def _(act):
        act.wait_ge(mk, 1)
        act.dma_start(w.sel[0:R0, :, R0:R0 + D], ins["L0_ffn_Wa_up"].rearrange("e r o -> r e o")).then_inc(ld2, 16)
        act.dma_start(w.sel[R0:R0 + 1, :, R0:R0 + D], ins["L0_ffn_ba_up"].rearrange("(a e) o -> a e o", a=1)
                      ).then_inc(ld2, 16)
        act.dma_start(w.sel[0:R0, :, R0 + D], ins["L0_ffn_ba_down"].rearrange("e r -> r e"),
                      allow_slow_non_contiguous=True).then_inc(ld2, 16)
        for k in range(3):
            act.dma_start(bd1[32 * k:32 * k + 1, :], ins["L0_ffn_bd1"].rearrange("(a e) h -> a (e h)", a=1)
                          ).then_inc(ld2, 16)
        act.dma_start(w.b2T[:, :], ins["L0_ffn_bd2"].rearrange("e d -> d e"),
                      allow_slow_non_contiguous=True).then_inc(ld2, 16)
        act.dma_start(base_at[R0:R0 + 1, :], ins["L0_ffn_b_base"].rearrange("(a o) -> a o", a=1)).then_inc(ld2, 16)

    @block.gpsimd
    def _(pool):
        pool.memset(bd1[:, :], 0.0)
        pool.memset(w.sel[:, :, R0:WSEL], 0.0).then_inc(mk, 1)
        pool.memset(w.ones3[:, :], 1.0)
        pool.memset(block_mask[:, :, :], 1.0)
        pool.memset(w.expert_mask[:, :, :], 0.0).then_inc(mk, 1)
        pool.wait_ge(mk, 2)
        pool.affine_select(out=block_mask[:, :, :], in_=block_mask[:, :, :], compare_op=ALU.is_ge, fill=0.0,
                           base=0, pattern=[[-H0, HALF], [0, H0]], channel_multiplier=1).then_inc(mk, 1)
        pool.wait_ge(mk, 3)
        pool.affine_select(out=block_mask[:, :, :], in_=block_mask[:, :, :], compare_op=ALU.is_ge, fill=0.0,
                           base=H0 - 1, pattern=[[H0, HALF], [0, H0]], channel_multiplier=-1).then_inc(mk, 1)
        pool.wait_ge(mk, 4)
        for half in range(2):
            last = pool.tensor_copy(w.expert_mask[:, half, half * HALF:(half + 1) * HALF], block_mask[:, :, 0])
        last.then_inc(mk, 1)
        pool.iota(w.down_count[:, :], pattern=[[1, E0]], base=-E0, channel_multiplier=0,
                  allow_small_or_imprecise_dtypes=True).then_inc(mk, 1)

    @block.tensor
    def _(pe):
        pe.wait_ge(g.consts_made, 3)
        pe.wait_ge(ld, 64)
        for half in range(2):
            last = pe.transpose(pT[:, half, 0:P], w2[:, half, :], g.identf[:, :])
        last.then_inc(tr, 1)
        pe.wait_ge(cp, 1)
        pe.wait_ge(ld2, 128)
        for half in range(2):
            pe.matmul(pW[:, half, 0:P], w2T[:, half, :], w2T[:, half, :], start=True, stop=True)
            last = pe.matmul(pB[:, half, 0:E0], w2T[:, half, :], w.b2T[:, :], start=True, stop=True)
        last.then_inc(mm, 1)

    @block.vector
    def _(dve):
        dve.wait_ge(ld, 64)
        dve.wait_ge(ld2, 128)
        dve.wait_ge(mk, 6)
        dve.tensor_copy(w.bd1_parts[:, :], bd1[:, :]).then_inc(bp, 1)
        dve.wait_ge(bp, 1)
        dve.tensor_tensor(bd1_rest[:, :], bd1[0:64, :], w.bd1_parts[0:64, :], ALU.subtract).then_inc(bp, 1)
        dve.wait_ge(bp, 2)
        dve.tensor_copy(w.bd1_parts[0:64, :], bd1_rest[:, :]).then_inc(bp, 1)
        dve.wait_ge(bp, 3)
        dve.tensor_tensor(w.bd1_parts[0:32, :], bd1_rest[0:32, :], w.bd1_parts[0:32, :], ALU.subtract)
        dve.tensor_tensor(w.sel[R0:R0 + 1, :, R0:R0 + D], w.sel[R0:R0 + 1, :, R0:R0 + D],
                          base_at[R0:R0 + 1, :].rearrange("p (a o) -> p a o", a=1).broadcast_to([1, E0, D]), ALU.add)
        dve.wait_ge(tr, 1)
        dve.tensor_copy(w2T[:, :, :], pT[:, :, 0:P]).then_inc(cp, 1)
        for half in range(2):
            x_cols = slice(P, P + D) if half == 0 else slice(0, D)
            dve.tensor_scalar(w.loss[:, half, x_cols], w2[:, half, :], -2.0, None, ALU.mult)
        dve.tensor_scalar(w.b2_slope[:, :], w.b2T[:, :], -2.0, None, ALU.mult)
        dve.scalar_tensor_tensor(out=w.b2_const[:, :], in0=w.b2T[:, :], scalar=float(L), in1=w.b2T[:, :],
                                 op0=ALU.mult, op1=ALU.mult)
        dve.wait_ge(mm, 1)
        for half in range(2):
            h_cols = slice(0, P) if half == 0 else slice(D + 1, LOSSCOL)
            one = P + D if half == 0 else D
            dve.tensor_tensor(w.loss[:, half, h_cols], pW[:, half, 0:P],
                              block_mask[:, :, :].rearrange("p e h -> p (e h)"), ALU.mult)
            dve.tensor_tensor_reduce(junk[:, :], pB[:, half, 0:E0], w.expert_mask[:, half, :], 2.0, 0.0,
                                     ALU.mult, ALU.add, w.loss[:, half, one:one + 1]).then_inc(st, 1)
            dve.wait_ge(st, half + 1)


def adapter_ffn(nc, g, w, sem, tag):
    s = record(**{n: sem(f"{tag}_{n}") for n in (
        "var", "rstd", "ones", "xn_ready", "xT_done", "xT_ready", "h_done", "h_ready", "gram_done", "score_ready",
        "loss_done",
        "adapter_ready", "a_done", "a_ready", "y_done", "y_free", "pick", "score")})
    with ExitStack() as ctx:
        def sb(name, shape):
            return ctx.enter_context(nc.sbuf_tensor(f"{tag}_{name}", shape, F32))

        def ps(name, shape):
            return ctx.enter_context(nc.psum_tensor(f"{tag}_{name}", shape, F32))

        hx = [sb(f"hx{i}", [P, NC, 2 * P + D + 1]) for i in range(2)]
        xT = [sb(f"xT{i}", [P, L]) for i in range(2)]
        picked = [sb(f"picked{i}", [P, WSEL]) for i in range(2)]
        aT = [sb(f"aT{i}", [R0 + 1, L]) for i in range(2)]
        junk = sb("junk", [P, 2, LOSSCOL])
        part = sb("part", [P, 2])
        score = sb("score", [P, E0])
        small = sb("small", [P, 4, E0])
        pT = ps("pT", [P, NC, P])
        pH = [ps(f"pH{i}", [P, 2, 2 * P]) for i in range(2)]
        pG = [ps(f"pG{i}", [P, 512]) for i in range(2)]
        pS = ps("pS", [P, 512])
        pA = ps("pA", [P, 512])
        pY = ps("pY", [P, NC, D])
        x_cols = slice(P, P + D)
        one_col = slice(P + D, P + D + 1)
        gram_cols = [slice(0, LOSSCOL), slice(P, P + LOSSCOL)]
        h_cols = [slice(0, P), slice(P + D + 1, 2 * P + D + 1)]
        block = ctx.enter_context(nc.Block())

        def over_steps(eng, step):
            step(0, None, 0)
            with eng.Fori(0, NB // 2 - 2) as i:
                step(2 * i + 1, 2 * i, 1)
                step(2 * i + 2, 2 * i + 1, 0)
            for b in range(NB - 3, NB):
                step(b, b - 1, b % 2)
            step(None, NB - 1, 0)

        def has_next(b, ahead):
            return b is not None and (not isinstance(b, int) or b + ahead < NB)

        @block.gpsimd
        def _(pool):
            def ones():
                for i in range(2):
                    pool.memset(hx[i][:, :, one_col], 1.0)
                    last = pool.memset(aT[i][:, :], 1.0)
                last.then_inc(s.ones, 1)

            take_rstd(pool, g, s.var, s.rstd, ones)

        @block.tensor
        def _(pe):
            pe.wait_ge(s.ones, 1)
            def transpose(b, par):
                pe.wait_ge(s.xn_ready, b + 1)
                for c in range(NC):
                    last = pe.transpose(pT[:, c, :], hx[par][:, c, x_cols], g.identf[:, :])
                last.then_inc(s.xT_done, 1)

            def step(new, old, par):
                if new is not None:
                    pe.wait_ge(s.xT_ready, new + 1)
                    for c in range(NC):
                        pe.matmul(pH[c // 2][:, c % 2, :], w.ones3[:, :], w.bd1_parts[:, :], start=True, stop=False)
                        last = pe.matmul(pH[c // 2][:, c % 2, :], xT[par][:, c * P:(c + 1) * P],
                                         w.wd1[:, :, :].rearrange("d e h -> d (e h)"), start=False, stop=True)
                        if c % 2:
                            last.then_inc(s.h_done, 1)
                    if has_next(new, 1):
                        transpose(new + 1, 1 - par)
                    pe.wait_ge(s.h_ready, 2 * new + 2)
                    for half in range(2):
                        for c in range(NC):
                            pe.matmul(pG[half][:, 0:LOSSCOL], hx[par][:, c, h_cols[half]],
                                      hx[par][:, c, gram_cols[half]], start=(c == 0), stop=(c == NC - 1))
                if old is not None:
                    pe.wait_ge(s.adapter_ready, old + 1)
                    pe.matmul(pA[0:R0, :], picked[1 - par][:, 0:R0], xT[1 - par][:, :],
                              start=True, stop=True).then_inc(s.a_done, 1)
                if new is not None:
                    for c in range(NC):
                        last = pe.matmul(pS[:, 0:1], hx[par][:, c, x_cols], hx[par][:, c, one_col],
                                         start=(c == 0), stop=(c == NC - 1))
                    last.then_inc(s.gram_done, 1)
                if old is not None:
                    pe.wait_ge(s.a_ready, old + 1)
                    pe.wait_ge(s.y_free, old + 1)
                    for c in range(NC):
                        pe.matmul(pY[:, c, :], xT[1 - par][:, c * P:(c + 1) * P], w.wbase[:, :],
                                  start=True, stop=False)
                        last = pe.matmul(pY[:, c, :], aT[1 - par][:, c * P:(c + 1) * P],
                                         picked[1 - par][0:R0 + 1, R0:R0 + D], start=False, stop=True)
                    last.then_inc(s.y_done, 1)
                if new is not None:
                    pe.wait_ge(s.score_ready, new + 1)
                    pe.matmul(pS[:, E0:2 * E0], g.onesf[:, :], score[:, :], start=True, stop=True
                              ).then_inc(s.loss_done, 1)

            transpose(0, 0)
            over_steps(pe, step)

        @block.scalar
        def _(act):
            def copy_transposed(b, par):
                act.wait_ge(s.xT_done, b + 1)
                act.copy(xT[par][:, :], pT[:, :, :].rearrange("p c t -> p (c t)")).then_inc(s.xT_ready, 1)

            def step(new, old, par):
                if new is not None:
                    for q in range(2):
                        act.wait_ge(s.h_done, 2 * new + q + 1)
                        for half in range(2):
                            last = act.activation(hx[par][:, 2 * q:2 * q + 2, h_cols[half]],
                                                  pH[q][:, :, half * P:(half + 1) * P], ACT.Relu)
                        last.then_inc(s.h_ready, 1)
                if old is not None:
                    act.wait_ge(s.a_done, old + 1)
                    act.activation(aT[1 - par][0:R0, :], pA[0:R0, :], ACT.Relu,
                                   bias=picked[1 - par][0:R0, R0 + D:WSEL]).then_inc(s.a_ready, 1)
                if has_next(new, 1):
                    if old is not None:
                        act.wait_ge(s.y_done, old + 1)
                    copy_transposed(new + 1, 1 - par)

            copy_transposed(0, 0)
            over_steps(act, step)

        @block.vector
        def _(dve):
            score_chain = Chain(dve, s.score, 3)
            pick_chain = Chain(dve, s.pick, 3 + E0 - 1)

            def norm(b, par):
                normalise(dve, g, b, hx[par][:, :, x_cols], s.rstd).then_inc(s.xn_ready, 1)

            def step(new, old, par):
                if new is not None:
                    dve.wait_ge(s.gram_done, new + 1)
                    score_chain.begin(new)
                    for half in range(2):
                        dve.tensor_tensor_reduce(junk[:, half, :], pG[half][:, 0:LOSSCOL], w.loss[:, half, :], 1.0,
                                                 0.0, ALU.mult, ALU.add, part[:, half:half + 1])
                    score_chain.link(dve.scalar_tensor_tensor(out=score[:, :], in0=w.b2_slope[:, :],
                                                              scalar=pS[:, 0:1], in1=w.b2_const[:, :],
                                                              op0=ALU.mult, op1=ALU.add))
                    score_chain.link(dve.scalar_tensor_tensor(out=score[:, :], in0=w.expert_mask[:, 0, :],
                                                              scalar=part[:, 0:1], in1=score[:, :],
                                                              op0=ALU.mult, op1=ALU.add))
                    dve.scalar_tensor_tensor(out=score[:, :], in0=w.expert_mask[:, 1, :], scalar=part[:, 1:2],
                                             in1=score[:, :], op0=ALU.mult, op1=ALU.add).then_inc(s.score_ready, 1)
                    if has_next(new, 2):
                        norm(new + 2, par)
                    dve.wait_ge(s.loss_done, new + 1)
                    pick_chain.begin(new)
                    loss = pS[:, E0:2 * E0]
                    score_chain.link(dve.tensor_reduce(small[:, 0, 0:1], loss, AX.X, ALU.min))
                    score_chain.end()
                    pick_chain.link(dve.scalar_tensor_tensor(out=small[:, 1, :], in0=loss, scalar=small[:, 0, 0:1],
                                                             in1=w.down_count[:, :], op0=ALU.is_equal, op1=ALU.mult))
                    pick_chain.link(dve.tensor_reduce(small[:, 0, 1:2], small[:, 1, :], AX.X, ALU.min))
                    pick_chain.link(dve.tensor_scalar(small[:, 2, :], w.down_count[:, :], small[:, 0, 1:2], None,
                                                      ALU.is_equal))
                    out = picked[par][:, :]
                    for e in range(E0):
                        if e == 0:
                            ins = dve.tensor_scalar(out, w.sel[:, e, :], small[:, 2, e:e + 1], None, ALU.mult)
                        else:
                            ins = dve.scalar_tensor_tensor(out=out, in0=w.sel[:, e, :], scalar=small[:, 2, e:e + 1],
                                                           in1=out, op0=ALU.mult, op1=ALU.add)
                        if e < E0 - 1:
                            pick_chain.link(ins)
                    pick_chain.end()
                    ins.then_inc(s.adapter_ready, 1)
                if old is not None:
                    dve.wait_ge(s.y_done, old + 1)
                    x = g.X[:, old]
                    dve.scalar_tensor_tensor(out=x, in0=pY[:, :, :], scalar=0.5, in1=x, op0=ALU.mult, op1=ALU.add
                                             ).then_inc(s.y_free, 1)
                    take_stats(dve, g, old, s.y_free, old + 2)

            dve.sem_inc(s.y_free, 1)
            take_variance(dve, g, s.var)
            dve.wait_ge(s.ones, 1)
            norm(0, 0)
            norm(1, 1)
            over_steps(dve, step)



NH, DH = 16, D // 16
GROUPS, GH = 4, 4
PAIRS = NH // 2
SCALE = float(D) ** -0.5
Q_PARTS = (0, 0, 0, 1, 1, 2)
K_PARTS = (0, 1, 2, 0, 1, 0)
STACK = len(Q_PARTS) * DH
LOAD_COUNT = 16 * 4
VW = 32


def attention_weights(block, ctx, nc, g, w, ins, sem):
    ld = sem("tw_loaded")
    mk = sem("tw_masked")
    tr = sem("tw_transposed")
    cp = sem("tw_copied")
    def sb(name, shape):
        return ctx.enter_context(nc.sbuf_tensor(name, shape, F32))

    wt, mask, masked = sb("tw_w", [P, 4, D]), sb("tw_m", [P, 4, D]), sb("tw_masked_w", [P, 4, D])
    bias, bias_mask = sb("tw_b", [1, D]), sb("tw_bm", [1, D])
    pT = ctx.enter_context(nc.psum_tensor("tw_pT", [P, 4, P], F32))

    @block.sync
    def _(sp):
        for dst, qkv, out in ((wt, "L0_attn_qkv_weight", "L0_attn_out_weight"),
                              (mask, "L0_attn_qkv_weight_mask", "L0_attn_out_weight_mask")):
            sp.dma_start(dst[:, 0:3, :], ins[qkv].rearrange("(j o) k -> o j k", o=P)).then_inc(ld, 16)
            sp.dma_start(dst[:, 3, :], ins[out]).then_inc(ld, 16)
        sp.dma_start(bias[:, :], ins["L0_attn_out_bias"].rearrange("(a o) -> a o", a=1)).then_inc(ld, 16)
        sp.dma_start(bias_mask[:, :], ins["L0_attn_out_bias_mask"].rearrange("(a o) -> a o", a=1)).then_inc(ld, 16)

    @block.vector
    def _(dve):
        dve.wait_ge(ld, 96)
        dve.scalar_tensor_tensor(out=masked[:, :, :], in0=mask[:, :, :], scalar=0.0, in1=wt[:, :, :],
                                 op0=ALU.is_gt, op1=ALU.mult).then_inc(mk, 1)
        dve.scalar_tensor_tensor(out=w.bo[:, :], in0=bias_mask[:, :], scalar=0.0, in1=bias[:, :],
                                 op0=ALU.is_gt, op1=ALU.mult)
        dve.wait_ge(tr, 1)
        dve.tensor_copy(w.wT[:, :, :], pT[:, :, :]).then_inc(cp, 1)

    @block.tensor
    def _(pe):
        pe.wait_ge(mk, 1)
        for j in range(4):
            last = pe.transpose(pT[:, j, :], masked[:, j, :], g.identf[:, :])
        last.then_inc(tr, 1)


Z_PLAN = [("max1", "seq", 0, "end"), ("xT", "next", 1, "mid"), ("out3", "prev", 1, "end"), ("q", "next", 2, "mid"),
      ("oT", "prev", 2, "end"), ("k", "next", 3, "mid"), ("y", "prev", 3, "end"), ("max2", "seq", 4, "end"),
      ("v", "next", 5, "mid"), ("out0", "seq", 5, "end"), ("max3", "seq", 8, "end"), ("out1", "seq", 9, "end"),
      ("max0", "next", 12, "end"), ("out2", "seq", 13, "end")]
Z_HEAD = ["xT", "q", "k", "v", "max0"]


def z_place(prev, seq, nxt):
    who = {"prev": prev, "seq": seq, "next": nxt}
    per = len(Z_PLAN)
    missing_first = sum(whose == "prev" for _, whose, _, _ in Z_PLAN)
    missing_last = sum(whose == "next" for _, whose, _, _ in Z_PLAN)
    if seq is None:
        at = len(Z_HEAD) + NB * per - missing_first - missing_last
    elif prev is None:
        at = len(Z_HEAD)
    else:
        at = seq * per + (len(Z_HEAD) - missing_first)
    out = {}
    for event, whose, slot, place in Z_PLAN:
        if who[whose] is not None:
            out[slot, place] = (event, who[whose], at)
            at = at + 1
    return out


def attention(nc, g, w, sem):
    s = record(**{n: sem(f"at_{n}") for n in (
        "var", "rstd", "xn_ready", "z_done", "q_high", "q_rest", "q_split", "q_out", "k_high", "k_rest", "k_split",
        "k_out", "v_ready", "va_in", "st_done", "exp_done", "pv_done", "o_free", "ao_ready", "x_done", "mx_done", "mx_free",
        "m_high", "m_rest", "m_split", "m_low", "m_out", "rden", "xT_ready", "oT_ready", "qk_low", "ones")})
    load_in = [sem(f"at_load{i}") for i in range(GROUPS)]
    m_in = [sem(f"at_m_in{i}") for i in range(GROUPS)]
    q_dram = nc.dram_tensor("q_stack", (NH, len(Q_PARTS), DH, L), BF16, kind="Internal").ap()
    k_dram = nc.dram_tensor("k_stack", (NH, len(K_PARTS), DH, L), BF16, kind="Internal").ap()
    m_dram = nc.dram_tensor("m_parts", (NH, 3, L), BF16, kind="Internal").ap()
    with ExitStack() as ctx:
        def sb(name, shape, dt=F32):
            return ctx.enter_context(nc.sbuf_tensor(f"at_{name}", shape, dt))

        def ps(name, shape):
            return ctx.enter_context(nc.psum_tensor(f"at_{name}", shape, F32))

        xn = sb("xn", [P, NC, D])
        xT = sb("xT", [P, L])
        qs, ks = sb("qs", [P, 3, L], BF16), sb("ks", [P, 3, L], BF16)
        qr, kr = sb("qr", [P, L]), sb("kr", [P, L])
        zero = sb("zero", [P, L])
        qq, kk = sb("qq", [P, PAIRS, L], BF16), sb("kk", [P, PAIRS, L], BF16)
        vt = sb("vt", [P, NC, D])
        va = sb("va", [P, NC, NH, VW])
        probs = sb("probs", [P, 2 * GH, L])
        nm = [sb(f"nm{i}", [P, NC, GH]) for i in range(2)]
        ms = sb("ms", [GH, 3, L], BF16)
        mr = sb("mr", [GH, L])
        os = sb("os", [P, L])
        rden = sb("rden", [P, NC, GH])
        ao = sb("ao", [P, NC, D])
        oT = sb("oT", [P, L])
        mx = [ps(f"mx{i}", [P, 2, L]) for i in range(2)]
        st = [ps(f"st{i}", [P, L]) for i in range(2)]
        po = ps("po", [P, L])
        z = ps("z", [P, L])
        z3 = z[:, :].rearrange("p (c d) -> p c d", c=NC)
        block = ctx.enter_context(nc.Block())

        def rows(h, n):
            return slice(64 * (h % 2), 64 * (h % 2) + n)

        def max_head(slot, seq, nxt):
            h = slot + 2 * GH
            return (seq, h) if h < NH else (nxt, h - NH)

        def over_all(eng, iteration):
            iteration(None, 0, 1)
            with eng.Fori(1, NB - 1) as b:
                iteration(b - 1, b, b + 1)
            iteration(NB - 2, NB - 1, None)
            iteration(NB - 1, None, None)

        @block.gpsimd
        def _(pool):
            def split(rest, parts, rest_sem, low_sem, split_sem, n):
                pool.wait_ge(rest_sem, n)
                pool.tensor_tensor(parts[:, 1, :], rest[:, :], zero[0:GH, :], ALU.add).then_inc(low_sem, 1)
                pool.wait_ge(low_sem, n)
                pool.tensor_tensor(parts[:, 2, :], rest[:, :], parts[:, 1, :], ALU.subtract).then_inc(split_sem, 1)

            def split_k(n):
                pool.wait_ge(s.k_rest, n)
                pool.tensor_tensor(ks[:, 1, :], kr[:, :], zero[:, :], ALU.add).then_inc(s.qk_low, 1)
                pool.wait_ge(s.qk_low, 2 * n)
                pool.tensor_tensor(ks[:, 2, :], kr[:, :], ks[:, 1, :], ALU.subtract).then_inc(s.k_split, 1)

            def split_q(n):
                if not isinstance(n, int) or n > 1:
                    pool.wait_ge(load_in[GROUPS - 1], LOAD_COUNT * (n - 1))
                pool.wait_ge(s.q_rest, n)
                pool.tensor_tensor(qs[:, 1, :], qr[:, :], zero[:, :], ALU.add).then_inc(s.qk_low, 1)
                pool.wait_ge(s.qk_low, 2 * n - 1)
                pool.tensor_tensor(qs[:, 2, :], qr[:, :], qs[:, 1, :], ALU.subtract).then_inc(s.q_split, 1)

            def split_max(seq, group):
                split(mr, ms, s.m_rest, s.m_low, s.m_split, seq * GROUPS + group + 1)

            def spread_values(seq, group):
                pool.wait_ge(s.v_ready, seq + 1)
                if not isinstance(seq, int) or seq > 0:
                    pool.wait_ge(s.pv_done, (seq - 1) * 16 + 4 * group + 4)
                heads = slice(group * GH, (group + 1) * GH)
                pool.tensor_tensor(
                    va[:, :, heads, 0:DH], vt[:, :, group * GH * DH:(group + 1) * GH * DH].rearrange(
                        "p c (h d) -> p c h d", h=GH),
                    zero[:, 0:NC * GH * DH].rearrange("p (c h d) -> p c h d", c=NC, h=GH), ALU.add
                ).then_inc(s.va_in, 1)

            def iteration(prev, seq, nxt):
                if seq is None:
                    return
                split_max(seq, 1)
                if prev is not None:
                    spread_values(seq, 3)
                if nxt is not None:
                    split_q(nxt + 1)
                    split_k(nxt + 1)
                split_max(seq, 2)
                if nxt is not None:
                    spread_values(nxt, 0)
                split_max(seq, 3)
                if nxt is not None:
                    spread_values(nxt, 1)
                    split_max(nxt, 0)
                    spread_values(nxt, 2)

            def head():
                pool.memset(zero[:, :], 0.0)
                pool.memset(kk[:, :, :], 1.0).then_inc(s.ones, 1)
                pool.wait_ge(s.ones, 1)
                split_q(1)
                split_k(1)
                pool.memset(va[:, :, :, :], 0.0).then_inc(s.ones, 1)
                pool.wait_ge(s.ones, 2)
                pool.memset(va[:, :, :, DH:DH + 1], 1.0).then_inc(s.ones, 1)

            take_rstd(pool, g, s.var, s.rstd, head)
            pool.wait_ge(s.ones, 3)
            for group in range(GROUPS):
                spread_values(0, group)
            split_max(0, 0)
            over_all(pool, iteration)

        @block.sync
        def _(sp):
            sp.wait_ge(s.ones, 1)

            def write_stacks(seq):
                for parts, ready, dram, order, out in ((qs, s.q_split, q_dram, Q_PARTS, s.q_out),
                                                       (ks, s.k_split, k_dram, K_PARTS, s.k_out)):
                    sp.wait_ge(ready, seq + 1)
                    for row, part in enumerate(order):
                        sp.dma_start(dram[:, row], parts[:, part, :]).then_inc(out, 16)

            def load(seq, group):
                if not isinstance(seq, int) or seq > 0:
                    sp.wait_ge(s.st_done, 64 * seq + 16 * (group + 1) - 64)
                if group == 0:
                    sp.wait_ge(s.q_out, 96 * seq + 96)
                    sp.wait_ge(s.k_out, 96 * seq + 96)
                pairs = slice(group * 2, group * 2 + 2)
                for dst, dram in ((qq, q_dram), (kk, k_dram)):
                    src = dram.rearrange("(p x) s d i -> x (s d) p i", x=2)
                    for half in range(2):
                        sp.dma_start(dst[64 * half:64 * half + STACK, pairs, :], src[half, :, pairs, :]
                                     ).then_inc(load_in[group], 16)

            def add_max(seq, group):
                sp.wait_ge(s.m_split, GROUPS * seq + group + 1)
                heads = slice(group * GH, (group + 1) * GH)
                sp.dma_start(m_dram[heads], ms[:, :, :]).then_inc(s.m_out, 16)
                sp.wait_ge(s.m_out, 16 * GROUPS * seq + 16 * (group + 1))
                src = m_dram.rearrange("(p x) s i -> x s p i", x=2)
                for half in range(2):
                    sp.dma_start(qq[64 * half + STACK:64 * half + STACK + 3, 2 * group:2 * group + 2, :],
                                 src[half, :, 2 * group:2 * group + 2, :]).then_inc(m_in[group], 16)

            def iteration(prev, seq, nxt):
                if seq is None:
                    return
                if prev is not None:
                    load(seq, 3)
                add_max(seq, 1)
                if nxt is not None:
                    write_stacks(nxt)
                add_max(seq, 2)
                if nxt is not None:
                    load(nxt, 0)
                add_max(seq, 3)
                if nxt is not None:
                    load(nxt, 1)
                    add_max(nxt, 0)
                    load(nxt, 2)

            write_stacks(0)
            for group in range(GROUPS):
                load(0, group)
            add_max(0, 0)
            over_all(sp, iteration)

        @block.tensor
        def _(pe):
            def take_z(last):
                if last is not None:
                    event, seq = last
                    name, n = event.rstrip("0123"), seq + 1
                    if event != name:
                        n = seq * GROUPS + int(event[-1]) + 1
                    read = {"xT": s.xT_ready, "q": s.q_rest, "k": s.k_rest, "v": s.v_ready, "max": s.m_rest,
                            "out": s.ao_ready, "oT": s.oT_ready, "y": s.x_done}[name]
                    pe.wait_ge(read, n)

            def z_event(event, seq, before):
                if event == "xT":
                    pe.wait_ge(s.xn_ready, seq + 1)
                    take_z(before)
                    for c in range(NC):
                        last = pe.transpose(z3[:, c, :], xn[:, c, :], g.identf[:, :])
                elif event in ("q", "k"):
                    if event == "q":
                        pe.wait_ge(s.xT_ready, seq + 1)
                    take_z(before)
                    last = pe.matmul(z[:, :], w.wT[:, "qk".index(event), :], xT[:, :], start=True, stop=True)
                elif event == "v":
                    take_z(before)
                    for c in range(NC):
                        last = pe.matmul(z3[:, c, :], xT[:, c * P:(c + 1) * P], w.wT[:, 2, :], start=True, stop=True)
                elif event.startswith("max"):
                    group = int(event[3])
                    pe.wait_ge(s.mx_free, seq * 32 + 8 * (group + 1))
                    take_z(before)
                    for c in range(NC):
                        last = pe.transpose(z3[0:GH, c, :], nm[group % 2][:, c, :], g.identf[:, :])
                elif event.startswith("out"):
                    pe.wait_ge(s.o_free, seq * GROUPS + int(event[3]) + 1)
                    take_z(before)
                    for c in range(NC):
                        last = pe.transpose(z3[:, c, :], os[:, c * P:(c + 1) * P], g.identf[:, :])
                elif event == "oT":
                    take_z(before)
                    for c in range(NC):
                        last = pe.transpose(z3[:, c, :], ao[:, c, :], g.identf[:, :])
                elif event == "y":
                    pe.wait_ge(s.oT_ready, seq + 1)
                    take_z(before)
                    for c in range(NC):
                        pe.matmul(z3[:, c, :], g.onesf[0:1, :], w.bo[:, :], start=True, stop=False)
                        last = pe.matmul(z3[:, c, :], oT[:, c * P:(c + 1) * P], w.wT[:, 3, :], start=False, stop=True)
                last.then_inc(s.z_done, 1)

            def max_scores(seq, h, half):
                n = 32 * seq + 2 * h + half
                if h % GH == 0 and half == 0:
                    pe.wait_ge(load_in[h // GH], LOAD_COUNT * (seq + 1))
                if not isinstance(n, int) or n > 1:
                    pe.wait_ge(s.mx_free, n - 1)
                for c in range(2):
                    q_at = (2 * half + c) * P
                    last = pe.matmul(mx[half][:, c, :], qq[rows(h, STACK), h // 2, q_at:q_at + P],
                                     kk[rows(h, STACK), h // 2, :], start=True, stop=True)
                last.then_inc(s.mx_done, 1)

            def scores(seq, slot, h4):
                group, tile = slot // 4, slot % 4
                h = group * GH + h4
                n = 64 * seq + 4 * slot + h4
                if tile == 0 and h4 == 0:
                    pe.wait_ge(m_in[group], 32 * (seq + 1))
                if not isinstance(n, int) or n > 1:
                    pe.wait_ge(s.exp_done, n - 1)
                pe.matmul(st[h4 % 2][:, :], kk[rows(h, STACK + 3), h // 2, tile * P:(tile + 1) * P],
                          qq[rows(h, STACK + 3), h // 2, :], start=True, stop=True).then_inc(s.st_done, 1)

            def values(seq, slot):
                group, tile = slot // 4, slot % 4
                pe.wait_ge(s.exp_done, 64 * seq + 4 * slot + 4)
                if tile == 0:
                    pe.wait_ge(s.va_in, GROUPS * seq + group + 1)
                    if not (isinstance(seq, int) and seq == 0 and group == 0):
                        pe.wait_ge(s.o_free, GROUPS * seq + group)
                for h4 in range(GH):
                    last = pe.matmul(po[VW * h4:VW * (h4 + 1), :], va[:, tile, group * GH + h4, :],
                                     probs[:, (slot % 2) * GH + h4, :], start=(tile == 0), stop=(tile == 3),
                                     skip_group_check=True)
                last.then_inc(s.pv_done, 1)

            def iteration(prev, seq, nxt):
                places = z_place(prev, seq, nxt)
                last = ("max0", 0) if prev is None else ("out2", prev)
                for slot in range(16):
                    m_seq, m_h = max_head(slot, seq, nxt)
                    if m_seq is not None:
                        max_scores(m_seq, m_h, 0)
                    if seq is not None:
                        scores(seq, slot, 0)
                        scores(seq, slot, 1)
                    if (slot, "mid") in places:
                        z_event(*places[slot, "mid"][:2], last)
                        last = places[slot, "mid"][:2]
                    if m_seq is not None:
                        max_scores(m_seq, m_h, 1)
                    if seq is not None:
                        scores(seq, slot, 2)
                        scores(seq, slot, 3)
                    if slot > 0 and seq is not None:
                        values(seq, slot - 1)
                    elif slot == 0 and prev is not None:
                        values(prev, 15)
                    if (slot, "end") in places:
                        z_event(*places[slot, "end"][:2], last)
                        last = places[slot, "end"][:2]

            for before, event in enumerate(Z_HEAD):
                if event == "max0":
                    for h in range(2 * GH):
                        for half in range(2):
                            max_scores(0, h, half)
                z_event(event, 0, (Z_HEAD[before - 1], 0) if before else None)
            over_all(pe, iteration)

        @block.scalar
        def _(act):
            def z_event(event, seq, before):
                if event == "xT":
                    act.wait_ge(s.z_done, before + 1)
                    act.copy(xT[:, :], z[:, :]).then_inc(s.xT_ready, 1)
                elif event in ("q", "k"):
                    parts, out, high = (qs, s.q_out, s.q_high) if event == "q" else (ks, s.k_out, s.k_high)
                    if not isinstance(seq, int) or seq > 0:
                        act.wait_ge(out, 96 * seq)
                    act.wait_ge(s.z_done, before + 1)
                    act.copy(parts[:, 0, :], z[:, :]).then_inc(high, 1)
                elif event == "v":
                    if not isinstance(seq, int) or seq > 0:
                        act.wait_ge(s.va_in, GROUPS * seq)
                    act.wait_ge(s.z_done, before + 1)
                    act.copy(vt[:, :, :], z3).then_inc(s.v_ready, 1)
                elif event.startswith("max"):
                    n = seq * GROUPS + int(event[3])
                    if not isinstance(n, int) or n > 0:
                        act.wait_ge(s.m_out, 16 * n)
                    act.wait_ge(s.z_done, before + 1)
                    act.copy(ms[:, 0, :], z[0:GH, :]).then_inc(s.m_high, 1)
                elif event == "oT":
                    act.wait_ge(s.z_done, before + 1)
                    act.copy(oT[:, :], z[:, :]).then_inc(s.oT_ready, 1)

            def take_output(seq, group):
                act.wait_ge(s.pv_done, 16 * seq + 4 * group + 4)
                act.copy(os[:, :], po[:, :]).then_inc(s.o_free, 1)

            def exponentials(seq, slot, h4):
                act.wait_ge(s.st_done, 64 * seq + 4 * slot + h4 + 1)
                act.activation(probs[:, (slot % 2) * GH + h4, :], st[h4 % 2][:, :], ACT.Exp, scale=SCALE
                               ).then_inc(s.exp_done, 1)

            def iteration(prev, seq, nxt):
                places = z_place(prev, seq, nxt)
                for slot in range(16):
                    if seq is not None:
                        exponentials(seq, slot, 0)
                        exponentials(seq, slot, 1)
                    if (slot, "mid") in places:
                        z_event(*places[slot, "mid"])
                    if seq is not None:
                        exponentials(seq, slot, 2)
                        exponentials(seq, slot, 3)
                    if slot == 0 and prev is not None:
                        take_output(prev, 3)
                    if slot % 4 == 0 and slot > 0 and seq is not None:
                        take_output(seq, slot // 4 - 1)
                    if (slot, "end") in places:
                        z_event(*places[slot, "end"])

            for before, event in enumerate(Z_HEAD):
                z_event(event, 0, before)
            over_all(act, iteration)

        @block.vector
        def _(dve):
            def z_event(event, seq, before):
                if event in ("q", "k"):
                    parts, rest, high, ready = ((qs, qr, s.q_high, s.q_rest) if event == "q" else
                                                (ks, kr, s.k_high, s.k_rest))
                    dve.wait_ge(high, seq + 1)
                    if not isinstance(seq, int) or seq > 0:
                        dve.wait_ge(s.q_split if event == "q" else s.k_split, seq)
                    dve.tensor_tensor(rest[:, :], z[:, :], parts[:, 0, :], ALU.subtract).then_inc(ready, 1)
                elif event.startswith("max"):
                    n = seq * GROUPS + int(event[3])
                    dve.wait_ge(s.m_high, n + 1)
                    if not isinstance(n, int) or n > 0:
                        dve.wait_ge(s.m_split, n)
                    dve.tensor_tensor(mr[:, :], z[0:GH, :], ms[:, 0, :], ALU.subtract).then_inc(s.m_rest, 1)
                elif event.startswith("out"):
                    group = int(event[3])
                    n = seq * GROUPS + group
                    dve.wait_ge(s.z_done, before + 1)
                    out4 = z[:, :].rearrange("p (c h v) -> p c h v", c=NC, h=GH)
                    dve.reciprocal(rden[:, :, :], out4[:, :, :, DH]).then_inc(s.rden, 1)
                    dve.wait_ge(s.rden, n + 1)
                    dve.tensor_tensor(
                        ao[:, :, group * GH * DH:(group + 1) * GH * DH].rearrange("p c (h d) -> p c h d", h=GH),
                        out4[:, :, :, 0:DH], rden[:, :, :].unsqueeze(3).broadcast_to([P, NC, GH, DH]), ALU.mult
                    ).then_inc(s.ao_ready, 1)
                elif event == "y":
                    dve.wait_ge(s.z_done, before + 1)
                    x = g.X[:, seq]
                    dve.tensor_tensor(x, z3, x, ALU.add).then_inc(s.x_done, 1)

            def row_max(seq, h, half):
                n = 32 * seq + 2 * h + half
                dve.wait_ge(s.mx_done, n + 1)
                dve.tensor_reduce(nm[(h // GH) % 2][:, 2 * half:2 * half + 2, h % GH], mx[half][:, :, :], AX.X,
                                  ALU.max, negate=True).then_inc(s.mx_free, 1)

            def iteration(prev, seq, nxt):
                places = z_place(prev, seq, nxt)
                for slot in range(16):
                    m_seq, m_h = max_head(slot, seq, nxt)
                    if m_seq is not None:
                        row_max(m_seq, m_h, 0)
                    if (slot, "mid") in places:
                        z_event(*places[slot, "mid"])
                    if m_seq is not None:
                        row_max(m_seq, m_h, 1)
                    if slot == 0 and nxt is not None:
                        normalise(dve, g, nxt, xn[:, :, :], s.rstd).then_inc(s.xn_ready, 1)
                    if (slot, "end") in places:
                        z_event(*places[slot, "end"])
                    if slot == 4 and prev is not None:
                        take_stats(dve, g, prev, s.x_done, prev + 1)

            take_variance(dve, g, s.var)
            normalise(dve, g, 0, xn[:, :, :], s.rstd).then_inc(s.xn_ready, 1)
            for before, event in enumerate(Z_HEAD):
                if event == "max0":
                    for h in range(2 * GH):
                        for half in range(2):
                            row_max(0, h, half)
                z_event(event, 0, before)
            over_all(dve, iteration)



E1, I1 = 8, 4 * D
NI = I1 // P
NT = NB * NC
COUNT_AT = 2
LOADS = 16 * 4
BIG = 3.0e38
COMBINE = 0.1


def moe_ffn(nc, g, ins, sem, tag, ahead=None, out=None):
    s = record(**{n: sem(f"{tag}_{n}") for n in (
        "var", "rstd", "w_in", "xn_ready", "xT_done", "xT_ready", "xT_stored", "logit_done", "logit_ready", "sig", "step",
        "counted", "shared_bias", "acc_done", "listed", "list_ready", "up_done", "gelu_done",
        "down_done", "shared_acc", "norm_step", "x_done", "x_out", "fin")})
    load_in = [sem(f"{tag}_load{i}") for i in range(2)]
    pD_free = [sem(f"{tag}_pD_free{i}") for i in range(2)]
    with ExitStack() as ctx:
        def sb(name, shape, dt=F32, to=ctx):
            return to.enter_context(nc.sbuf_tensor(f"{tag}_{name}", shape, dt))

        def ps(name, shape, to):
            return to.enter_context(nc.psum_tensor(f"{tag}_{name}", shape, F32))

        xT_all = sb("xT_all", [P, NB, L])
        acc = sb("acc", [P, NT, D])
        logit = sb("logit", [P, NT, E1])
        w8 = sb("w8", [P, NT, E1])
        w_listed = sb("w_listed", [P, NT, E1])
        listed = sb("listed", [1, E1], mybir.dt.int32)
        pairs = sb("pairs", [1, 1], mybir.dt.int32)
        down_b = [sb(f"down_b{i}", [P, D]) for i in range(2)]
        up = [sb(f"up{i}", [P, I1]) for i in range(2)]
        up_b = [sb(f"up_b{i}", [P, NI]) for i in range(2)]
        down = [sb(f"down{i}", [P, NI, D]) for i in range(2)]

        def row_to_all(row):
            return row.rearrange("(a h) -> a h", a=1).broadcast_to([P, D])

        with ExitStack() as c1:
            gate = sb("gate", [P, E1], to=c1)
            gate_b = sb("gate_b", [P, E1], to=c1)
            xn = [sb(f"xn{i}", [P, NC, D], to=c1) for i in range(2)]
            xT = [sb(f"xT{i}", [P, L], to=c1) for i in range(2)]
            pT = [ps(f"pT{i}", [P, NC, P], c1) for i in range(2)]
            pL = [ps(f"pL{i}", [P, 512], c1) for i in range(2)]
            block = c1.enter_context(nc.Block())

            @block.sync
            def _(sp):
                sp.dma_start(gate[:, :], ins["L1_ffn_gate_w"]).then_inc(s.w_in, 16)
                sp.dma_start(gate_b[:, :], ins["L1_ffn_bias"].rearrange("(a e) -> a e", a=1).broadcast_to([P, E1])
                             ).then_inc(s.w_in, 16)
                sp.dma_start(up[0][:, :], ins["L1_ffn_sw_up"]).then_inc(load_in[0], 16)
                sp.dma_start(down[0][:, :, :], ins["L1_ffn_sw_down"].rearrange("(k i) h -> i k h", i=P)
                             ).then_inc(load_in[0], 16)
                sp.dma_start(up_b[0][:, :], ins["L1_ffn_sb_up"].rearrange("(k i) -> i k", i=P),
                             allow_slow_non_contiguous=True).then_inc(load_in[0], 16)
                sp.dma_start(down_b[0][:, :], row_to_all(ins["L1_ffn_sb_down"])).then_inc(load_in[0], 16)
                if ahead is not None:
                    load_scan_weights(sp, ahead, ins)

            @block.gpsimd
            def _(pool):
                take_rstd(pool, g, s.var, s.rstd)

            @block.tensor
            def _(pe):
                pe.wait_ge(s.w_in, 32)

                def step(new, old, par):
                    if new is not None:
                        pe.wait_ge(s.xn_ready, new + 1)
                        pe.wait_ge(s.logit_ready, new + 1)
                        for c in range(NC):
                            last = pe.transpose(pT[par][:, c, :], xn[par][:, c, :], g.identf[:, :])
                        last.then_inc(s.xT_done, 1)
                    if old is not None:
                        pe.wait_ge(s.xT_ready, old + 1)
                        for c in range(NC):
                            last = pe.matmul(pL[1 - par][:, c * E1:(c + 1) * E1], xT[1 - par][:, c * P:(c + 1) * P],
                                             gate[:, :], start=True, stop=True)
                        last.then_inc(s.logit_done, 1)

                over_sequences(pe, step)

            @block.scalar
            def _(act):
                def step(new, old, par):
                    if new is not None:
                        act.wait_ge(s.xT_done, new + 1)
                        act.copy(xT[par][:, :], pT[par][:, :, :].rearrange("p c t -> p (c t)")
                                 ).then_inc(s.xT_ready, 1)

                over_sequences(act, step)

            @block.vector
            def _(dve):
                dve.sem_inc(s.logit_ready, 2)
                take_variance(dve, g, s.var)
                dve.wait_ge(s.w_in, 32)

                def step(new, old, par):
                    if new is not None and not (isinstance(new, int) and new == NB - 1):
                        if old is not None:
                            dve.wait_ge(s.xT_done, old + 1)
                        normalise(dve, g, new + 1, xn[1 - par][:, :, :], s.rstd).then_inc(s.xn_ready, 1)
                    if old is not None:
                        dve.wait_ge(s.xT_ready, old + 1)
                        dve.tensor_scalar(xT_all[:, old, :], pT[1 - par][:, :, :].rearrange("p c t -> p (c t)"), 1.0,
                                          None, ALU.mult).then_inc(s.xT_stored, 1)
                        dve.wait_ge(s.logit_done, old + 1)
                        dve.tensor_tensor(logit[:, :, :].rearrange("p (b c) e -> p b c e", b=NB)[:, old, :, :],
                                          pL[1 - par][:, 0:NC * E1].rearrange("p (c e) -> p c e", c=NC),
                                          gate_b[:, :].unsqueeze(1).broadcast_to([P, NC, E1]), ALU.add
                                          ).then_inc(s.logit_ready, 1)

                normalise(dve, g, 0, xn[0][:, :, :], s.rstd).then_inc(s.xn_ready, 1)
                over_sequences(dve, step)

        with ExitStack() as c2:
            ramp = sb("ramp", [P, E1], to=c2)
            index = sb("index", [1, E1], to=c2)
            sig = sb("sig", [P, NT, E1], to=c2)
            z2 = sb("z2", [P, NT, E1], to=c2)
            eq = sb("eq", [P, NT, E1], to=c2)
            hot = [sb(f"hot{i}", [P, NT, E1], to=c2) for i in range(2)]
            top = sb("top", [P, NT], to=c2)
            den = sb("den", [P, NT], to=c2)
            count = sb("count", [P, E1], to=c2)
            key = sb("key", [P, E1], to=c2)
            less = sb("less", [P, E1, E1], to=c2)
            rank = sb("rank", [P, E1], to=c2)
            place = sb("place", [P, E1, E1], to=c2)
            order = sb("order", [P, NT, E1, E1], to=c2)
            entry = sb("entry", [1, E1, E1], to=c2)
            listf = sb("listf", [1, E1], to=c2)
            pairsf = sb("pairsf", [1, 1], to=c2)
            more = sb("more", [1, 2], to=c2)
            limits = sb("limits", [1, 2], to=c2)
            hidden = [sb(f"hidden{i}", [P, NI, L], to=c2) for i in range(2)]
            most = sb("most", [P, NT], to=c2)
            pU = [ps(f"pU{i}", [P, L], c2) for i in range(NI)]
            pD = [ps(f"pD{i}", [P, NC, D], c2) for i in range(2)]
            pC = ps("pC", [P, 512], c2)
            out_b = [sb(f"out_b{i}", [P, NC, D], to=c2) for i in range(2)]
            block = c2.enter_context(nc.Block())

            def listed_experts(eng, expert):
                eng.wait_ge(s.list_ready, 1)
                trips = eng.value_load(pairs[0:1, 0:1], min_val=1, max_val=E1 // 2 - 1)
                with eng.Fori(0, trips) as i:
                    expert(2 * i + 1, 1, 2 * i, i, False)
                    expert(2 * i + 2, 0, 2 * i + 1, i, False)
                expert(2 * trips + 1, 1, 2 * trips, trips, False)
                expert(2 * trips + 2, 0, 2 * trips + 1, trips, True)

            @block.sync
            def _(sp):
                def expert(n, buf, place, trip, is_last):
                    e = sp.value_load(listed[0:1, bass.ds(place, 1)], min_val=0, max_val=E1 - 1)
                    sp.wait_ge(s.down_done, NB * n - NB + 2)
                    sp.dma_start(up[buf][:, :], ins["L1_ffn_up_w"][e]).then_inc(load_in[buf], 16)
                    sp.dma_start(down[buf][:, :, :], ins["L1_ffn_down_w"][e].rearrange("(k i) h -> i k h", i=P)
                                 ).then_inc(load_in[buf], 16)
                    sp.dma_start(up_b[buf][:, :], ins["L1_ffn_up_b"][e].rearrange("(k i) -> i k", i=P),
                                 allow_slow_non_contiguous=True).then_inc(load_in[buf], 16)
                    sp.dma_start(down_b[buf][:, :], row_to_all(ins["L1_ffn_down_b"][e])).then_inc(load_in[buf], 16)

                listed_experts(sp, expert)
                if out is not None:
                    for b in range(NB):
                        sp.wait_ge(s.x_done, b + 1)
                        sp.dma_start(out[b].rearrange("(c p) d -> p c d", p=P), g.X[:, b]).then_inc(s.x_out, 16)
                    sp.wait_ge(s.x_out, 16 * NB)

            @block.gpsimd
            def _(pool):
                pool.iota(ramp[:, :], pattern=[[-1, E1]], base=E1, channel_multiplier=0,
                          allow_small_or_imprecise_dtypes=True).then_inc(s.fin, 1)
                pool.wait_ge(s.fin, 1)
                pool.iota(index[:, :], pattern=[[1, E1]], base=0, channel_multiplier=0,
                          allow_small_or_imprecise_dtypes=True).then_inc(s.fin, 1)
                pool.wait_ge(s.fin, 2)
                pool.iota(limits[:, :], pattern=[[2, 2]], base=4, channel_multiplier=0,
                          allow_small_or_imprecise_dtypes=True).then_inc(s.fin, 1)
                if ahead is not None:
                    make_scan_constants(pool, g, ahead)

            @block.scalar
            def _(act):
                act.activation(sig[:, :, :], logit[:, :, :], ACT.Sigmoid).then_inc(s.sig, 1)

                def gelus(n, buf, t):
                    for k in range(NI):
                        act.wait_ge(s.up_done, NI * (NB * n + t) + k + 1)
                        act.activation(hidden[t % 2][:, k, :], pU[k][:, :], ACT.Gelu, bias=up_b[buf][:, k:k + 1]
                                       ).then_inc(s.gelu_done, 1)

                for t in range(NB + 1):
                    if t < NB:
                        gelus(0, 0, t)
                    if t > 0:
                        act.wait_ge(s.down_done, t)
                        act.copy(acc[:, (t - 1) * NC:t * NC, :], pD[(t - 1) % 2][:, :, :]).then_inc(s.shared_acc, 1)

                def expert(n, buf, place, trip, is_last):
                    for t in range(NB):
                        gelus(n, buf, t)

                listed_experts(act, expert)

            @block.vector
            def _(dve):
                chain = Chain(dve, s.step, 31)
                chain.begin(0)
                link = chain.link

                def wide(tile):
                    return tile[:, :].unsqueeze(2).broadcast_to([P, NT, E1])

                def per_expert(row):
                    return row[:, :].unsqueeze(1).broadcast_to([P, NT, E1])

                dve.wait_ge(s.fin, 3)
                for i, z in enumerate((logit, z2)):
                    link(dve.tensor_reduce(top[:, :], z[:, :, :], AX.X, ALU.max))
                    link(dve.tensor_tensor(eq[:, :, :], z[:, :, :], wide(top), ALU.is_equal))
                    link(dve.tensor_tensor(eq[:, :, :], eq[:, :, :], per_expert(ramp), ALU.mult))
                    link(dve.tensor_reduce(top[:, :], eq[:, :, :], AX.X, ALU.max))
                    link(dve.tensor_tensor(hot[i][:, :, :], per_expert(ramp), wide(top), ALU.is_equal))
                    if i == 0:
                        link(dve.scalar_tensor_tensor(out=z2[:, :, :], in0=hot[0][:, :, :], scalar=-BIG,
                                                      in1=logit[:, :, :], op0=ALU.mult, op1=ALU.add))
                link(dve.tensor_tensor(hot[0][:, :, :], hot[0][:, :, :], hot[1][:, :, :], ALU.add))
                dve.wait_ge(s.sig, 1)
                link(dve.tensor_tensor(sig[:, :, :], sig[:, :, :], hot[0][:, :, :], ALU.mult))
                link(dve.tensor_reduce(den[:, :], sig[:, :, :], AX.X, ALU.add))
                link(dve.tensor_scalar(den[:, :], den[:, :], 1e-6, None, ALU.add))
                link(dve.reciprocal(den[:, :], den[:, :]))
                link(dve.tensor_tensor(w8[:, :, :], sig[:, :, :], wide(den), ALU.mult))
                link(dve.tensor_reduce(count[:, :], hot[0][:, :, :].rearrange("p t e -> p e t"), AX.X, ALU.add))
                dve.wait_ge(s.counted, 1)
                link(dve.tensor_scalar(key[:, :], pC[:, 0:E1], 0.0, -float(E1), ALU.is_gt, ALU.mult))
                link(dve.tensor_reduce(pairsf[:, :], key[0:1, :], AX.X, ALU.add))
                link(dve.tensor_scalar(pairsf[:, :], pairsf[:, :], -1.0 / E1, None, ALU.mult))
                link(dve.tensor_tensor(more[:, :], limits[:, :], pairsf[:, :].broadcast_to([1, 2]), ALU.is_lt))
                link(dve.tensor_reduce(pairsf[:, :], more[:, :], AX.X, ALU.add))
                link(dve.tensor_scalar(pairs[:, :], pairsf[:, :], 1.0, None, ALU.add))
                link(dve.tensor_tensor(key[:, :], key[:, :], ramp[:, :], ALU.subtract))
                link(dve.tensor_tensor(less[:, :, :], key[:, :].unsqueeze(1).broadcast_to([P, E1, E1]),
                                       key[:, :].unsqueeze(2).broadcast_to([P, E1, E1]), ALU.is_lt))
                link(dve.tensor_reduce(rank[:, :], less[:, :, :], AX.X, ALU.add))
                link(dve.tensor_scalar(rank[:, :], rank[:, :], -1.0, float(E1), ALU.mult, ALU.add))
                link(dve.tensor_tensor(place[:, :, :], ramp[:, :].unsqueeze(2).broadcast_to([P, E1, E1]),
                                       rank[:, :].unsqueeze(1).broadcast_to([P, E1, E1]), ALU.is_equal))
                link(dve.tensor_tensor(entry[:, :, :], place[0:1, :, :],
                                       index[:, :].unsqueeze(1).broadcast_to([1, E1, E1]), ALU.mult))
                link(dve.tensor_reduce(listf[:, :], entry[:, :, :], AX.X, ALU.add))
                chain.end()
                dve.tensor_copy(listed[:, :], listf[:, :]).then_inc(s.list_ready, 1)
                for r in range(E1):
                    last = dve.tensor_tensor(order[:, :, r, :], w8[:, :, :],
                                             place[:, r, :].unsqueeze(1).broadcast_to([P, NT, E1]), ALU.mult)
                last.then_inc(s.listed, 1)
                dve.wait_ge(s.listed, 1)
                dve.tensor_reduce(w_listed[:, :, :], order[:, :, :, :], AX.X, ALU.add)
                dve.wait_ge(load_in[0], LOADS)
                for b in range(NB):
                    tiles = slice(b * NC, (b + 1) * NC)
                    dve.wait_ge(s.shared_acc, b + 1)
                    dve.tensor_tensor(acc[:, tiles, :], acc[:, tiles, :],
                                      down_b[0][:, :].unsqueeze(1).broadcast_to([P, NC, D]), ALU.add
                                      ).then_inc(s.shared_bias, 1)
                dve.wait_ge(s.shared_bias, NB)
                for half in range(2):
                    dve.sem_inc(pD_free[half], 1)

                norm = Chain(dve, s.norm_step, 4)

                def finish(b):
                    tiles = slice(b * NC, (b + 1) * NC)
                    norm.begin(b)
                    norm.link(dve.tensor_reduce(most[:, tiles], acc[:, tiles, :], AX.X, ALU.max,
                                                apply_absolute_value=True))
                    norm.link(dve.tensor_scalar(most[:, tiles], most[:, tiles], COMBINE, 1e-6, ALU.mult, ALU.add))
                    norm.link(dve.reciprocal(most[:, tiles], most[:, tiles]))
                    norm.link(dve.tensor_scalar(most[:, tiles], most[:, tiles], 0.5 * COMBINE, None, ALU.mult))
                    norm.end()
                    for c in range(NC):
                        x = g.X[:, b, c, :]
                        last = dve.scalar_tensor_tensor(out=x, in0=acc[:, b * NC + c, :],
                                                        scalar=most[:, b * NC + c:b * NC + c + 1], in1=x,
                                                        op0=ALU.mult, op1=ALU.add)
                    last.then_inc(s.x_done, 1)
                    if out is None:
                        take_stats(dve, g, b, s.x_done, b + 1)

                def expert(n, buf, place, trip, is_last):
                    dve.wait_ge(load_in[buf], LOADS * (trip + 2 - buf))
                    for t in range(NB):
                        dve.wait_ge(s.down_done, NB * n + t + 1)
                        dve.tensor_tensor(out_b[t % 2][:, :, :], pD[t % 2][:, :, :],
                                          down_b[buf][:, :].unsqueeze(1).broadcast_to([P, NC, D]), ALU.add
                                          ).then_inc(pD_free[t % 2], 1)
                        dve.wait_ge(pD_free[t % 2], NB // 2 * n - NB // 2 + t // 2 + 2)
                        for c in range(NC):
                            at = acc[:, t * NC + c, :]
                            last = dve.scalar_tensor_tensor(
                                out=at, in0=out_b[t % 2][:, c, :],
                                scalar=w_listed[:, t * NC + c, bass.ds(place, 1)], in1=at,
                                op0=ALU.mult, op1=ALU.add)
                        if is_last:
                            last.then_inc(s.acc_done, 1)
                            dve.wait_ge(s.acc_done, t + 1)
                            finish(t)

                listed_experts(dve, expert)

            @block.tensor
            def _(pe):
                def up_product(n, buf, t):
                    m = NB * n + t
                    for k in range(NI):
                        if not isinstance(m, int) or m > 0:
                            pe.wait_ge(s.gelu_done, NI * m + k + 1 - NI)
                        pe.matmul(pU[k][:, :], up[buf][:, k * P:(k + 1) * P], xT_all[:, t, :],
                                  start=True, stop=True).then_inc(s.up_done, 1)

                def down_product(n, buf, t):
                    pe.wait_ge(s.gelu_done, NI * (NB * n + t) + NI)
                    for c in range(NC):
                        for k in range(NI):
                            last = pe.matmul(pD[t % 2][:, c, :], hidden[t % 2][:, k, c * P:(c + 1) * P],
                                             down[buf][:, k, :], start=(k == 0), stop=(k == NI - 1))
                    last.then_inc(s.down_done, 1)

                pe.wait_ge(load_in[0], LOADS)
                for t in range(NB + 1):
                    if t == COUNT_AT:
                        pe.wait_ge(s.step, 18)
                        pe.matmul(pC[:, 0:E1], g.onesf[:, :], count[:, :], start=True, stop=True).then_inc(s.counted, 1)
                    if t < NB:
                        up_product(0, 0, t)
                    if t > 0:
                        if t > 2:
                            pe.wait_ge(s.shared_acc, t - 2)
                        down_product(0, 0, t - 1)

                def expert(n, buf, place, trip, is_last):
                    pe.wait_ge(load_in[buf], LOADS * (trip + 2 - buf))
                    for t in range(NB + 1):
                        if t < NB:
                            up_product(n, buf, t)
                        if t == 1:
                            pe.wait_ge(s.shared_acc, NB)
                        if t > 0:
                            pe.wait_ge(pD_free[(t - 1) % 2], NB // 2 * n - NB // 2 + (t - 1) // 2 + 1)
                            down_product(n, buf, t - 1)

                listed_experts(pe, expert)



NS = 16
RT = 64
RING = 4
LEAD = 3
QROWS = 32


def scan_weights(sb, sem):
    return record(
        kT=sb("ss_kT", [P, 3]), dcoef=sb("ss_dcoef", [P, 1]), a_log=sb("ss_a_log", [P, NS]),
        w_bc=sb("ss_w_bc", [P, 3, QROWS]), b_bc=sb("ss_b_bc", [3 * QROWS, 1]), w_dt=sb("ss_w_dt", [P, RT]),
        b_dt=sb("ss_b_dt", [RT, 1]), w_dtp=sb("ss_w_dtp", [RT, D]), b_dtp=sb("ss_b_dtp", [P, 1]),
        diag_k=sb("ss_diag_k", [P, 3, P]), diag_d=sb("ss_diag_d", [P, P]), pick=sb("ss_pick", [3 * QROWS, QROWS]),
        select=sb("ss_select", [3 * QROWS, QROWS, P], BF16), loaded=sem("ss_w_in"), made=sem("ss_made"))


def load_scan_weights(sp, q, ins):
    def column(a):
        return a.rearrange("(p a) -> p a", a=1)

    sp.dma_start(q.kT[:, :], ins["L1_attn_conv_kernel"].rearrange("k a d -> d (k a)"),
                 allow_slow_non_contiguous=True).then_inc(q.loaded, 16)
    sp.dma_start(q.dcoef[:, :], column(ins["L1_attn_Dcoeff"]), allow_slow_non_contiguous=True).then_inc(q.loaded, 16)
    sp.dma_start(q.a_log[:, :], ins["L1_attn_A_log"]).then_inc(q.loaded, 16)
    for k in range(3):
        sp.dma_start(q.w_bc[:, k, :], ins["L1_attn_W_bc"]).then_inc(q.loaded, 16)
        sp.dma_start(q.b_bc[k * QROWS:(k + 1) * QROWS, :], column(ins["L1_attn_b_bc"]),
                     allow_slow_non_contiguous=True).then_inc(q.loaded, 16)
    sp.dma_start(q.w_dt[:, :], ins["L1_attn_W_dt"]).then_inc(q.loaded, 16)
    sp.dma_start(q.w_dtp[:, :], ins["L1_attn_W_dtp"]).then_inc(q.loaded, 16)
    sp.dma_start(q.b_dt[:, :], column(ins["L1_attn_b_dt"]), allow_slow_non_contiguous=True).then_inc(q.loaded, 16)
    sp.dma_start(q.b_dtp[:, :], column(ins["L1_attn_b_dtp"]), allow_slow_non_contiguous=True).then_inc(q.loaded, 16)


def make_scan_constants(pool, g, q):
    pool.memset(q.pick[:, :], 0.0).then_inc(q.made, 1)
    for k in range(3):
        pool.wait_ge(q.made, k + 1)
        pool.affine_select(out=q.pick[:, :], in_=q.pick[:, :], compare_op=ALU.not_equal, fill=1.0,
                           base=-k * QROWS, pattern=[[-1, QROWS]], channel_multiplier=1).then_inc(q.made, 1)
    pool.wait_ge(q.made, 4)
    pool.tensor_copy(q.select[:, :, :], q.pick[:, :].unsqueeze(2).broadcast_to([3 * QROWS, QROWS, P]))
    pool.wait_ge(q.loaded, 13 * 16)
    for k in range(3):
        pool.tensor_scalar(q.diag_k[:, k, :], g.identf[:, :], q.kT[:, k:k + 1], None, ALU.mult)
    pool.tensor_scalar(q.diag_d[:, :], g.identf[:, :], q.dcoef[:, :], None, ALU.mult).then_inc(q.made, 1)


def selective_scan(nc, g, q, sem, tag):
    s = record(**{n: sem(f"{tag}_{n}") for n in (
        "var", "rstd", "xn_ready", "xT_done", "xT_ready", "u_done", "e_ready", "e1_ready", "inv", "us_ready",
        "bc_done", "bc_ready", "dt1_ready", "lin_done", "w_ready", "ln_ready", "e_dt", "nd_ready", "r_ready",
        "rest_ready", "mid_ready", "split_ready", "corr_ready", "dt_ready", "xdt_ready", "b_bcast", "c_bcast",
        "c_ready", "alpha_ready",
        "beta", "h_ready", "hc_ready", "hc_used", "y_free", "zeros_made", "a_made")})
    with ExitStack() as ctx:
        def sb(name, shape, dt=F32):
            return ctx.enter_context(nc.sbuf_tensor(f"{tag}_{name}", shape, dt))

        def ps(name, shape):
            return ctx.enter_context(nc.psum_tensor(f"{tag}_{name}", shape, F32))

        a_pos, a_neg, zeros = sb("a_pos", [P, NS]), sb("a_neg", [P, NS]), sb("zeros", [1, P + L], BF16)
        xn = [sb(f"xn{i}", [P, NC, D]) for i in range(2)]
        xT = [sb(f"xT{i}", [P, L + 2]) for i in range(2)]
        parts = [sb(f"parts{i}", [3 * QROWS, L], BF16) for i in range(2)]
        dt = [sb(f"dt_of{i}", [P, L]) for i in range(2)]
        xdt = [sb(f"xdt{i}", [P, L]) for i in range(2)]
        e, e1, inv, us = (sb(n, [P, L]) for n in ("e", "e1", "inv", "us"))
        bc, bc_rest, dt1 = sb("bc", [3 * QROWS, L]), sb("bc_rest", [2 * QROWS, L]), sb("dt_low", [RT, L])
        edt, w1, lnw, nd, rw, corr = (sb(n, [P, L]) for n in ("edt", "w1", "lnw", "nd", "rw", "corr"))
        alpha, beta, h, c_sb, hc = (
            [sb(f"{n}{i}", [P, L]) for i in range(RING)] for n in ("alpha", "beta", "h", "c", "hc"))

        pF = [ps(f"pF{i}", [P, L]) for i in range(2)]
        pB = [ps(f"pB{i}", [P, L]) for i in range(2)]
        pC = [ps(f"pC{i}", [P, L]) for i in range(2)]
        pY = [ps(f"pY{i}", [P, NC, D]) for i in range(2)]

        def over_steps(eng, step):
            step(0, None, None, 0)
            step(1, 0, None, 1)
            with eng.Fori(0, NB // 2 - 1) as i:
                step(2 * i + 2, 2 * i + 1, 2 * i, 0)
                step(2 * i + 3, 2 * i + 2, 2 * i + 1, 1)
            step(None, NB - 1, NB - 2, 0)
            step(None, None, NB - 1, 1)

        def wait_for(eng, sem_, b, n):
            if not (isinstance(b, int) and b * NS + n < 0):
                eng.wait_ge(sem_, b * NS + n + 1)

        block = ctx.enter_context(nc.Block())

        @block.gpsimd
        def _(pool):
            def zero_columns():
                pool.memset(xT[0][:, :], 0.0)
                pool.memset(xT[1][:, :], 0.0)
                pool.memset(zeros[:, :], 0.0).then_inc(s.zeros_made, 1)

            take_rstd(pool, g, s.var, s.rstd, zero_columns)

            def inputs(b, par, n):
                if n == 9:
                    pool.wait_ge(s.bc_ready, b + 1)
                    pool.tensor_tensor(bc_rest[:, :], bc[0:2 * QROWS, :], parts[par][0:2 * QROWS, :], ALU.subtract
                                       ).then_inc(s.rest_ready, 1)
                if n == 11:
                    pool.wait_ge(s.corr_ready, b + 1)
                    pool.tensor_tensor(dt[par][:, :], lnw[:, :], corr[:, :], ALU.subtract).then_inc(s.dt_ready, 1)
                if n == 13:
                    pool.wait_ge(s.mid_ready, b + 1)
                    pool.tensor_tensor(parts[par][0:QROWS, :], bc_rest[0:QROWS, :], parts[par][0:QROWS, :],
                                       ALU.subtract).then_inc(s.split_ready, 1)

            def step(new, old, older, par):
                for n in range(NS):
                    if new is not None:
                        inputs(new, par, n)
                    if old is not None:
                        wait_for(pool, s.h_ready, old, n)
                        wait_for(pool, s.c_ready, old, n)
                        wait_for(pool, s.hc_used, old, n - RING)
                        pool.tensor_tensor(hc[n % RING][:, :], h[n % RING][:, :], c_sb[n % RING][:, :], ALU.mult
                                           ).then_inc(s.hc_ready, 1)

            over_steps(pool, step)

        @block.tensor
        def _(pe):
            pe.wait_ge(s.zeros_made, 1)

            def inputs(b, par, n):
                if n == 1:
                    pe.wait_ge(s.xn_ready, b + 1)
                    for c in range(NC):
                        last = pe.transpose(pF[0][:, c * P:(c + 1) * P], xn[par][:, c, :], g.identf[:, :])
                    last.then_inc(s.xT_done, 1)
                if n in (3, 4):
                    pe.wait_ge(s.xT_ready, b + 1)
                    for k in ((0, 1) if n == 3 else (2,)):
                        last = pe.matmul(pF[1][:, :], q.diag_k[:, k, :], xT[par][:, k:k + L],
                                         start=(k == 0), stop=(k == 2))
                    if n == 4:
                        last.then_inc(s.u_done, 1)
                if n == 6:
                    pe.wait_ge(s.us_ready, b + 1)
                    pe.matmul(pF[0][0:3 * QROWS, :], q.w_bc[:, :, :].rearrange("d k r -> d (k r)"), us[:, :],
                              start=True, stop=True)
                    pe.matmul(pF[1][0:RT, :], q.w_dt[:, :], us[:, :], start=True, stop=True).then_inc(s.bc_done, 1)
                if n == 8:
                    pe.wait_ge(s.dt1_ready, b + 1)
                    pe.wait_ge(s.bc_ready, b + 1)
                    pe.matmul(pF[0][:, :], q.w_dtp[:, :], dt1[:, :], start=True, stop=True).then_inc(s.lin_done, 1)

            def broadcast(b, par, n):
                if n == 0:
                    pe.wait_ge(s.split_ready, b + 1)
                wait_for(pe, s.beta, b, n - 2)
                pe.matmul(pB[n % 2][:, :], q.select[:, n, :], parts[par][:, :], start=True, stop=True
                          ).then_inc(s.b_bcast, 1)
                wait_for(pe, s.c_ready, b, n - 2)
                pe.matmul(pC[n % 2][:, :], q.select[:, NS + n, :], parts[par][:, :], start=True, stop=True
                          ).then_inc(s.c_bcast, 1)

            def add_state(b, par, n):
                if n == 0:
                    pe.wait_ge(s.y_free, b + 1)
                    pe.matmul(pY[par][:, :, :], zeros[:, 0:P], zeros[:, P:P + L], start=True, stop=False)
                    for c in range(NC):
                        pe.matmul(pY[par][:, c, :], xT[par][:, 1 + c * P:1 + (c + 1) * P], q.diag_d[:, :],
                                  start=False, stop=False)
                wait_for(pe, s.hc_ready, b, n)
                for c in range(NC):
                    last = pe.matmul(pY[par][:, c, :], hc[n % RING][:, c * P:(c + 1) * P], g.identf[:, :],
                                     start=False, stop=(n == NS - 1 and c == NC - 1))
                last.then_inc(s.hc_used, 1)

            def step(new, old, older, par):
                for n in range(NS):
                    if old is not None:
                        broadcast(old, 1 - par, n)
                    if new is not None:
                        inputs(new, par, n)
                    if n < LEAD and older is not None:
                        add_state(older, par, NS - LEAD + n)
                    if n >= LEAD and old is not None:
                        add_state(old, 1 - par, n - LEAD)

            over_steps(pe, step)

        @block.scalar
        def _(act):
            act.preload_act_table_set("natural_log_exp_and_others")
            act.activation(a_pos[:, :], q.a_log[:, :], ACT.Exp).then_inc(s.a_made, 1)
            act.wait_ge(s.a_made, 1)
            act.activation(a_neg[:, :], a_pos[:, :], ACT.Identity, scale=-1.0).then_inc(s.a_made, 1)
            act.wait_ge(s.a_made, 2)

            def inputs(b, par, n):
                if n == 2:
                    act.wait_ge(s.xT_done, b + 1)
                    act.copy(xT[par][:, 1:L + 1], pF[0][:, :]).then_inc(s.xT_ready, 1)
                if n == 4:
                    act.wait_ge(s.u_done, b + 1)
                    act.activation(e[:, :], pF[1][:, :], ACT.Exp, scale=-1.0).then_inc(s.e_ready, 1)
                    act.wait_ge(s.e_ready, b + 1)
                    act.activation(e1[:, :], e[:, :], ACT.Ln, bias=1.0).then_inc(s.e1_ready, 1)
                    act.wait_ge(s.e1_ready, b + 1)
                    act.activation(inv[:, :], e1[:, :], ACT.Exp, scale=-1.0).then_inc(s.inv, 1)
                if n == 7:
                    act.wait_ge(s.bc_done, b + 1)
                    act.activation(dt1[:, :], pF[1][0:RT, :], ACT.Identity, bias=q.b_dt[:, :]).then_inc(s.dt1_ready, 1)
                    act.activation(parts[par][:, :], pF[0][0:3 * QROWS, :], ACT.Identity, bias=q.b_bc[:, :])
                    act.activation(bc[:, :], pF[0][0:3 * QROWS, :], ACT.Identity, bias=q.b_bc[:, :]
                                   ).then_inc(s.bc_ready, 1)
                if n == 9:
                    act.wait_ge(s.lin_done, b + 1)
                    act.activation(edt[:, :], pF[0][:, :], ACT.Exp, bias=q.b_dtp[:, :]).then_inc(s.e_dt, 1)
                    act.wait_ge(s.e_dt, b + 1)
                    act.activation(w1[:, :], edt[:, :], ACT.Identity, bias=1.0).then_inc(s.w_ready, 1)
                if n == 10:
                    act.wait_ge(s.w_ready, b + 1)
                    act.activation(lnw[:, :], w1[:, :], ACT.Ln).then_inc(s.ln_ready, 1)
                if n == 11:
                    act.wait_ge(s.ln_ready, b + 1)
                    act.activation(rw[:, :], lnw[:, :], ACT.Exp, scale=-1.0).then_inc(s.r_ready, 1)
                if n == 12:
                    act.wait_ge(s.rest_ready, b + 1)
                    act.copy(parts[par][0:2 * QROWS, :], bc_rest[:, :]).then_inc(s.mid_ready, 1)

            def step(new, old, older, par):
                for n in range(NS):
                    if new is not None:
                        inputs(new, par, n)
                    if old is not None:
                        if n == 0:
                            act.wait_ge(s.dt_ready, old + 1)
                        wait_for(act, s.h_ready, old, n - RING)
                        act.activation(alpha[n % RING][:, :], dt[1 - par][:, :], ACT.Exp, scale=a_neg[:, n:n + 1]
                                       ).then_inc(s.alpha_ready, 1)
                        wait_for(act, s.c_bcast, old, n)
                        wait_for(act, s.hc_ready, old, n - RING)
                        act.copy(c_sb[n % RING][:, :], pC[n % 2][:, :]).then_inc(s.c_ready, 1)

            over_steps(act, step)

        @block.vector
        def _(dve):
            dve.sem_inc(s.y_free, 2)
            take_variance(dve, g, s.var)

            def inputs(b, par, n):
                if n == 0:
                    normalise(dve, g, b, xn[par], s.rstd).then_inc(s.xn_ready, 1)
                if n == 5:
                    dve.wait_ge(s.inv, b + 1)
                    dve.tensor_tensor(us[:, :], pF[1][:, :], inv[:, :], ALU.mult).then_inc(s.us_ready, 1)
                if n == 11:
                    dve.wait_ge(s.w_ready, b + 1)
                    dve.scalar_tensor_tensor(out=nd[:, :], in0=w1[:, :], scalar=-1.0, in1=edt[:, :],
                                             op0=ALU.add, op1=ALU.subtract).then_inc(s.nd_ready, 1)
                if n == 12:
                    dve.wait_ge(s.nd_ready, b + 1)
                    dve.wait_ge(s.r_ready, b + 1)
                    dve.tensor_tensor(corr[:, :], nd[:, :], rw[:, :], ALU.mult).then_inc(s.corr_ready, 1)
                if n == 14:
                    dve.wait_ge(s.dt_ready, b + 1)
                    dve.tensor_tensor(xdt[par][:, :], xT[par][:, 1:L + 1], dt[par][:, :], ALU.mult
                                      ).then_inc(s.xdt_ready, 1)

            def scan(b, n):
                wait_for(dve, s.beta, b, n)
                wait_for(dve, s.alpha_ready, b, n)
                wait_for(dve, s.hc_ready, b, n - RING)
                dve.tensor_tensor_scan(h[n % RING][:, :], alpha[n % RING][:, :], beta[n % RING][:, :], 0.0,
                                       ALU.mult, ALU.add).then_inc(s.h_ready, 1)

            def step(new, old, older, par):
                for n in range(NS):
                    if new is not None:
                        inputs(new, par, n)
                    if n == LEAD + 1 and older is not None:
                        wait_for(dve, s.hc_used, older, NS - 1)
                        dve.tensor_tensor(g.X[:, older, :, :], g.X[:, older, :, :], pY[par][:, :, :], ALU.add
                                          ).then_inc(s.y_free, 1)
                        take_stats(dve, g, older, s.y_free, older + 3)
                    if old is not None:
                        if n == 0:
                            dve.wait_ge(s.xdt_ready, old + 1)
                        wait_for(dve, s.b_bcast, old, n)
                        wait_for(dve, s.h_ready, old, n - RING)
                        dve.tensor_tensor(beta[n % RING][:, :], pB[n % 2][:, :], xdt[1 - par][:, :], ALU.mult
                                          ).then_inc(s.beta, 1)
                        if n:
                            scan(old, n - 1)
                if old is not None:
                    scan(old, NS - 1)

            over_steps(dve, step)


def macaron(nc, ins, out):
    with ExitStack() as ctx:
        def sb(name, shape, dt=F32):
            return ctx.enter_context(nc.sbuf_tensor(name, shape, dt))

        taken = []

        def sem(name):
            taken.append(nc.alloc_semaphore(name=name))
            return taken[-1]

        g = record(
            X=sb("X", [P, NB, NC, D]), mean=sb("mean", [P, NB, NC]), rstd=sb("rstd", [P, NB, NC]),
            ln_t=sb("ln_t", [P, NB, NC]), ln_u=sb("ln_u", [P, NB, NC]), bn6=sb("bn6", [P, NB, NC, 6]),
            carrier=sb("carrier", [P, NB, 1]), consts_made=sem("consts_made"), identf=sb("identf", [P, P]),
            onesf=sb("onesf", [P, P]), neghalf=sb("neghalf", [P, NB, NC]))
        w = record(
            wd1=sb("wd1", [P, E0, H0]), bd1_parts=sb("bd1_parts", [BIAS_ROWS, E0 * H0], BF16),
            ones3=sb("ones3", [BIAS_ROWS, P], BF16), wbase=sb("wbase", [P, D]),
            sel=sb("adapters", [P, E0, WSEL]), b2T=sb("b2T", [P, E0]), b2_slope=sb("b2_slope", [P, E0]),
            b2_const=sb("b2_const", [P, E0]), loss=sb("loss_weights", [P, 2, LOSSCOL]),
            expert_mask=sb("expert_mask", [P, 2, E0]), down_count=sb("down_count", [P, E0]),
            wT=sb("wT", [P, 4, D]), bo=sb("bo", [1, D]))
        with ExitStack() as start:
            block = start.enter_context(nc.Block())
            set_up(block, g, ins, sem)
            adapter_weights(block, start, nc, g, w, ins, sem)
            attention_weights(block, start, nc, g, w, ins, sem)
        adapter_ffn(nc, g, w, sem, "f1")
        attention(nc, g, w, sem)
        nc.all_engine_barrier()
        nc.clear_and_free_semaphores(taken)
        nc.all_engine_barrier()
        adapter_ffn(nc, g, w, sem, "f2")
        q = scan_weights(sb, sem)
        moe_ffn(nc, g, ins, sem, "m1", ahead=q)
        selective_scan(nc, g, q, sem, "ss")
        moe_ffn(nc, g, ins, sem, "m2", out=out)


_INS = ['L0_attn_x', 'L0_attn_qkv_weight', 'L0_attn_qkv_weight_mask', 'L0_attn_out_weight', 'L0_attn_out_weight_mask',
        'L0_attn_out_bias', 'L0_attn_out_bias_mask', 'L0_ffn_W_base', 'L0_ffn_b_base', 'L0_ffn_Wd1', 'L0_ffn_bd1',
        'L0_ffn_Wd2', 'L0_ffn_bd2', 'L0_ffn_Wa_down', 'L0_ffn_ba_down', 'L0_ffn_Wa_up', 'L0_ffn_ba_up',
        'L1_attn_conv_kernel', 'L1_attn_A_log', 'L1_attn_W_bc', 'L1_attn_b_bc', 'L1_attn_Dcoeff', 'L1_attn_W_dt',
        'L1_attn_b_dt', 'L1_attn_W_dtp', 'L1_attn_b_dtp', 'L1_ffn_gate_w', 'L1_ffn_bias', 'L1_ffn_up_w', 'L1_ffn_up_b',
        'L1_ffn_down_w', 'L1_ffn_down_b', 'L1_ffn_sw_up', 'L1_ffn_sb_up', 'L1_ffn_sw_down', 'L1_ffn_sb_down']
_OUTS = [((NB, L, D), 'float32')]


def kernel(**inputs):
    import numpy as _np
    import concourse.bacc as _bacc
    from concourse import mybir as _mybir
    from concourse.bass_utils import run_bass_kernel_spmd as _run

    nc = _bacc.Bacc("TRN2", target_bir_lowering=False, num_devices=1)
    arrays, ins = {}, {}
    for name in _INS:
        a = _np.ascontiguousarray(inputs[name])
        arrays[f"in_{name}_dram"] = a
        ins[name] = nc.dram_tensor(f"in_{name}_dram", a.shape, _mybir.dt.from_np(a.dtype), kind="ExternalInput").ap()
    shape, dtype = _OUTS[0]
    out = nc.dram_tensor("out_0_dram", shape, _mybir.dt.from_np(_np.dtype(dtype)), kind="ExternalOutput").ap()
    macaron(nc, ins, out)
    r = _run(nc, [arrays], core_ids=[0])
    return r.results[0]["out_0_dram"]
```
